# Optimizing a Trainium2 kernel written in Bass

```python
import numpy as np
import jax
import jax.numpy as jnp

def _softmax(x, axis=-1):
    return jax.nn.softmax(x, axis=axis)

def _gelu(x):
    return jax.nn.gelu(x, approximate=True)

def _silu(x):
    return jax.nn.silu(x)

def _sigmoid(x):
    return jax.nn.sigmoid(x)

def _layernorm(x, axis=-1, eps=1e-05):
    m = jnp.mean(x, axis=axis, keepdims=True)
    v = jnp.var(x, axis=axis, keepdims=True)
    return (x - m) / jnp.sqrt(v + eps)

def _scatter_add(tgt, idx, src, axis=0):
    return tgt.at[idx].add(src)

def _segment_sum(src, seg, n):
    return jax.ops.segment_sum(src, seg, n)
kernel_name = 'mk_xattn_ffn_d1_seqx_r4_1661cc'

def setup_inputs(seed: int=0):
    np.random.seed(seed)
    _w = jnp.asarray

    def _rec_inputs():
        import jax
        import jax.numpy as jnp
        _rk = jax.random.key(seed)
        x = -0.0002928 + 1 * jax.random.normal(jax.random.fold_in(_rk, 1), (4, 512, 256), jnp.float32)
        _lenS = 512 - jax.random.randint(jax.random.fold_in(_rk, 7), (4,), 0, max(1, 512 // 4) + 1, jnp.int32)
        _lenS2 = 512 - jax.random.randint(jax.random.fold_in(_rk, 8), (4,), 0, max(1, 512 // 4) + 1, jnp.int32)
        _ctx_1024P = jax.random.normal(jax.random.fold_in(_rk, 11), (4, 16, 256), jnp.float32)
        _ctx_1024c = jax.random.dirichlet(jax.random.fold_in(_rk, 511), 0.3 * jnp.ones((16,), jnp.float32), (4, 512))
        _ctx_1024t = jnp.einsum('bsk,bkd->bsd', _ctx_1024c, _ctx_1024P)
        _ctx_1024t = _ctx_1024t * jax.lax.rsqrt(jnp.mean(jnp.square(_ctx_1024t)) + 1e-12) * 0.953939
        ctx_1024 = -1.39393e-06 + 0.999914 * (_ctx_1024t + 0.3 * jax.random.normal(jax.random.fold_in(_rk, 611), (4, 512, 256), jnp.float32))
        _validS = jnp.arange(512)[None, :] < _lenS[:, None]
        _validS2 = jnp.arange(512)[None, :] < _lenS2[:, None]
        _causal = jnp.tril(jnp.ones((512, 512), dtype=bool))
        mask_Bx1xSxS2_ik1 = jnp.where(jnp.broadcast_to(_validS2[:, None, None, :], (4, 1, 512, 512)), 1, 0).astype(jnp.int32)
        return (x, ctx_1024, mask_Bx1xSxS2_ik1)
    x, ctx_1024, mask_Bx1xSxS2_ik1 = _rec_inputs()

    def _L0_xattn_setup():
        import jax, jax.numpy as jnp
        import numpy as np
        B, S, E, H = (2, 512, 256, 16)
        D = E // H
        key = jax.random.key(seed)
        ks = jax.random.split(key, 14)
        inp = {'query': jax.random.normal(ks[0], (B, S, E), jnp.float32), 'key': jax.random.normal(ks[1], (B, S, E), jnp.float32), 'value': jax.random.normal(ks[2], (B, S, E), jnp.float32), 'adj': jax.random.normal(ks[3], (S, S), jnp.float32), 'mask': jax.random.randint(ks[4], (B, 1, S, S), 0, 2, jnp.int32)}
        sc = 1.0 / np.sqrt(E)
        inp['Wq'] = jax.random.normal(ks[5], (E, E), jnp.float32) * sc
        inp['bq'] = jax.random.normal(ks[6], (E,), jnp.float32) * sc
        inp['Wk'] = jax.random.normal(ks[7], (E, E), jnp.float32) * sc
        inp['bk'] = jax.random.normal(ks[8], (E,), jnp.float32) * sc
        inp['Wv'] = jax.random.normal(ks[9], (E, E), jnp.float32) * sc
        inp['bv'] = jax.random.normal(ks[10], (E,), jnp.float32) * sc
        inp['Wo'] = jax.random.normal(ks[11], (E, E), jnp.float32) * sc
        inp['bo'] = jax.random.normal(ks[12], (E,), jnp.float32) * sc
        return inp
    _L0_xattn_all = _L0_xattn_setup()
    _L0_xattn_in = {k: v for k, v in _L0_xattn_all.items() if k in ('adj', 'Wq', 'bq', 'Wk', 'bk', 'Wv', 'bv', 'Wo', 'bo')}
    del _L0_xattn_all

    def _L0_ffn_setup():
        import jax, jax.numpy as jnp
        import numpy as np
        E = 16
        F_C = 2.0
        D = 256
        I = 4 * D
        IS = 2 * D
        B, S = (4, 256)
        key = jax.random.key(seed)
        ks = jax.random.split(key, 8)
        w = 0.02
        return {'hidden_states': jax.random.normal(ks[0], (B, S, D), dtype=jnp.float32), 'gate_w': jax.random.normal(ks[1], (E, D), dtype=jnp.float32) * w, 'Wg': jax.random.normal(ks[2], (E, I, D), dtype=jnp.float32) * w, 'Wu': jax.random.normal(ks[3], (E, I, D), dtype=jnp.float32) * w, 'Wd': jax.random.normal(ks[4], (E, D, I), dtype=jnp.float32) * w, 'Sg': jax.random.normal(ks[5], (IS, D), dtype=jnp.float32) * w, 'Su': jax.random.normal(ks[6], (IS, D), dtype=jnp.float32) * w, 'Sd': jax.random.normal(ks[7], (D, IS), dtype=jnp.float32) * w}
    _L0_ffn_all = _L0_ffn_setup()
    _L0_ffn_in = {k: v for k, v in _L0_ffn_all.items() if k in ('gate_w', 'Wg', 'Wu', 'Wd', 'Sg', 'Su', 'Sd')}
    del _L0_ffn_all
    return {'x': x, 'ctx_1024': ctx_1024, 'mask_Bx1xSxS2_ik1': mask_Bx1xSxS2_ik1, 'L0_xattn_adj': _L0_xattn_in['adj'], 'L0_xattn_Wq': _L0_xattn_in['Wq'], 'L0_xattn_bq': _L0_xattn_in['bq'], 'L0_xattn_Wk': _L0_xattn_in['Wk'], 'L0_xattn_bk': _L0_xattn_in['bk'], 'L0_xattn_Wv': _L0_xattn_in['Wv'], 'L0_xattn_bv': _L0_xattn_in['bv'], 'L0_xattn_Wo': _L0_xattn_in['Wo'], 'L0_xattn_bo': _L0_xattn_in['bo'], 'L0_ffn_gate_w': _L0_ffn_in['gate_w'], 'L0_ffn_Wg': _L0_ffn_in['Wg'], 'L0_ffn_Wu': _L0_ffn_in['Wu'], 'L0_ffn_Wd': _L0_ffn_in['Wd'], 'L0_ffn_Sg': _L0_ffn_in['Sg'], 'L0_ffn_Su': _L0_ffn_in['Su'], 'L0_ffn_Sd': _L0_ffn_in['Sd']}

def reference(x, ctx_1024, mask_Bx1xSxS2_ik1, L0_xattn_adj, L0_xattn_Wq, L0_xattn_bq, L0_xattn_Wk, L0_xattn_bk, L0_xattn_Wv, L0_xattn_bv, L0_xattn_Wo, L0_xattn_bo, L0_ffn_gate_w, L0_ffn_Wg, L0_ffn_Wu, L0_ffn_Wd, L0_ffn_Sg, L0_ffn_Su, L0_ffn_Sd):
    import jax
    import jax.numpy as jnp

    def _L0_xattn_ref(query, key, value, adj, mask, Wq, bq, Wk, bk, Wv, bv, Wo, bo):
        import jax, jax.numpy as jnp
        import numpy as np
        B, S, E, H = (2, 512, 256, 16)
        D = E // H
        b, s, _ = query.shape

        def heads(x, W, bias):
            y = jnp.einsum('bse,ef->bsf', x, W.T) + bias
            return y.reshape(b, s, H, D).transpose(0, 2, 1, 3)
        Q = heads(query, Wq, bq)
        K = heads(key, Wk, bk)
        V = heads(value, Wv, bv)
        scores = jnp.einsum('bhqd,bhkd->bhqk', Q, K) / jnp.sqrt(jnp.float32(D))
        scores = scores + adj[None, None, :, :]
        scores = jnp.where(mask == 0, jnp.float32(-jnp.inf), scores)
        weights = jax.nn.softmax(scores, axis=-1)
        out = jnp.einsum('bhqk,bhkd->bhqd', weights, V)
        out = out.transpose(0, 2, 1, 3).reshape(b, s, E)
        return jnp.einsum('bse,ef->bsf', out, Wo.T) + bo

    def _L0_ffn_ref(hidden_states, gate_w, Wg, Wu, Wd, Sg, Su, Sd):
        import jax, jax.numpy as jnp
        import numpy as np
        E = 16
        F_C = 2.0
        D = 256
        I = 4 * D
        IS = 2 * D
        B, S = (4, 256)
        b, s, d = hidden_states.shape
        T = b * s
        C = int(T * F_C / E)
        flat_x = hidden_states.reshape(T, d)
        logits = flat_x @ gate_w.T
        scores = jax.nn.softmax(logits, axis=-1).T
        topk_weight, topk_idx = jax.lax.top_k(scores, C)
        xg = flat_x[topk_idx]
        g = jnp.einsum('ecd,eid->eci', xg, Wg)
        u = jnp.einsum('ecd,eid->eci', xg, Wu)
        h = jax.nn.gelu(g, approximate=False) * u
        eo = jnp.einsum('eci,edi->ecd', h, Wd)
        eo = eo * topk_weight[..., None]
        flat_out = jnp.zeros_like(flat_x).at[topk_idx.reshape(-1)].add(eo.reshape(-1, d))
        out = flat_out.reshape(b, s, d)
        sg = hidden_states @ Sg.T
        su = hidden_states @ Su.T
        shared = jax.nn.gelu(sg, approximate=False) * su @ Sd.T
        return out + shared
    x = x + _L0_xattn_ref(_layernorm(x, axis=-1), ctx_1024, ctx_1024, L0_xattn_adj, mask_Bx1xSxS2_ik1, L0_xattn_Wq, L0_xattn_bq, L0_xattn_Wk, L0_xattn_bk, L0_xattn_Wv, L0_xattn_bv, L0_xattn_Wo, L0_xattn_bo)
    x = x + _L0_ffn_ref(_layernorm(x, axis=-1), L0_ffn_gate_w, L0_ffn_Wg, L0_ffn_Wu, L0_ffn_Wd, L0_ffn_Sg, L0_ffn_Su, L0_ffn_Sd)
    return x

_drawn_inputs = setup_inputs


def setup_inputs(seed=0):
    import zlib

    import numpy as np

    out = dict(_drawn_inputs(seed))
    spreads = {}
    factors = {'L0_xattn_bq': 4.276,
     'L0_xattn_bk': 64.0,
     'L0_ffn_gate_w': 8.0,
     'L0_ffn_Wg': 8.0,
     'L0_ffn_Wu': 8.0,
     'L0_ffn_Wd': 8.0,
     'L0_ffn_Sg': 8.0,
     'L0_ffn_Su': 8.0,
     'L0_ffn_Sd': 8.0}
    for name, (base, spread) in spreads.items():
        noise = np.random.default_rng([zlib.crc32(name.encode()), seed]).standard_normal(out[name].shape)
        drawn = base * np.exp(spread * noise) if base else spread * noise
        out[name] = jnp.asarray(drawn.astype(out[name].dtype))
    for name, factor in factors.items():
        out[name] = (out[name] * factor).astype(out[name].dtype)
    return out
```

```python
from contextlib import ExitStack

import concourse.bass as bass
from concourse import mybir

ALU = mybir.AluOpType
ACT = mybir.ActivationFunctionType
F32 = mybir.dt.float32
BF16 = mybir.dt.bfloat16
I32 = mybir.dt.int32
U32 = mybir.dt.uint32
AX = mybir.AxisListType

P = 128
EPS = 1e-5
MASKED = 1e30
LARGEST = 3e38

Q_PART = [0, 0, 1, 1, 0, 2]
K_PART = [0, 1, 0, 1, 2, 0]
PT_RING = 5
QK_RING = 3
M_BANKS = 3


class Job:

    def __init__(self, step, kind, b, i, engine):
        self.step, self.kind, self.b, self.i, self.engine = step, kind, b, i, engine


def plan_jobs(B, first):
    jobs = []
    for b in range(B):
        at = 64 * (b - 1)
        steps = [8, 9, 12, 16, 20, 24, 28, 30, 32, 34] if b else [68 - 14 + i for i in range(10)]
        kinds = [("xT", 0, "act"), ("xT", 1, "act"), ("q", 0, "dve"), ("k", 0, "dve"), ("q", 1, "dve"),
                 ("k", 1, "dve"), ("v", 0, "dve"), ("v", 1, "dve"), ("v", 2, "dve"), ("v", 3, "dve")]
        for step, (kind, i, engine) in zip(steps, kinds):
            jobs.append(Job(at + step, kind, b, i, engine))
        for g in range(4):
            jobs.append(Job(64 * b + 16 * (g + 1) + 9.5, "norm", b, g, "dve"))
        at = 64 * (b + 1)
        for i, step in enumerate([11, 13]):
            jobs.append(Job(at + step, "aT", b, i, "act"))
        for i, step in enumerate([15, 17, 18, 19]):
            jobs.append(Job(at + step, "y", b, i, "dve"))
        for i, step in enumerate([27, 29]):
            jobs.append(Job(at + step, "xn2T", b, i, "act"))
        jobs.append(Job(at + 31, "lg", b, 0, "dve"))
        for i in range(4):
            jobs.append(Job(at + 36 + 4 * i, "sg", b, i, "act"))
            jobs.append(Job(at + 38 + 4 * i, "su", b, i, "dve"))
        for i, step in enumerate([53, 55, 57, 59]):
            jobs.append(Job(at + step, "dn", b, i, "dve"))
    jobs.sort(key=lambda j: j.step)
    done = {"act": 0, "dve": 0}
    for n, j in enumerate(jobs):
        j.n = n
        j.step = int(j.step)
        done[j.engine] += 1
        j.done = done[j.engine]
    return jobs


def build(nc, x, ctxT, mask, adj, WqT, bq, WkT, bk, WvT, bv, WoT, bo, gateT, WgT, WuT, WdT,
          SgT, SuT, SdT, out, PHASES=3):
    T, D = x.shape
    B = mask.shape[0]
    S = T // B
    H = 16
    DH = D // H
    E = gateT.shape[1]
    I = WgT.shape[2]
    IS = SgT.shape[1]
    C = 2 * T // E
    NT = T // P
    QT = S // P
    DC = D // P
    UNITS = B * H * QT
    FIRST = -16
    LAST = UNITS + 64

    x_v = x.rearrange("(n p) d -> p n d", p=P)
    out_v = out.rearrange("(n p) d -> p n d", p=P)

    jobs = plan_jobs(B, FIRST)
    job = {(j.kind, j.b, j.i): j for j in jobs}

    norms = sorted([(64 * (b - 1) + (4 if b else 48), 1, b) for b in range(B)]
                   + [(64 * (b + 1) + 21, 2, b) for b in range(B)])
    norm_n = {(which, b): n for n, (_, which, b) in enumerate(norms)}

    with ExitStack() as ctx:
        def sb(name, shape, dt, stack=ctx):
            return stack.enter_context(nc.sbuf_tensor(name, shape, dt))

        def sem(name):
            return ctx.enter_context(nc.semaphore(name))

        qk_d = nc.dram_tensor("qk_parts", [B, 2, 3, D, S], BF16, kind="Internal").ap()
        xn2_d = nc.dram_tensor("xn2_rows", [T, D], F32, kind="Internal").ap()

        ps_s = [ctx.enter_context(nc.psum_tensor(f"ps_s{i}", [P, 512], F32)) for i in range(2)]
        ps_t = [ctx.enter_context(nc.psum_tensor(f"ps_t{i}", [P, 512], F32)) for i in range(2)]
        ps_u = ctx.enter_context(nc.psum_tensor("ps_u", [P, 512], F32))
        ps_m = [ctx.enter_context(nc.psum_tensor(f"ps_m{i}", [P, 512], F32)) for i in range(M_BANKS)]

        ident = sb("ident", [P, P], F32)
        logits = sb("logits", [P, NT, E], F32)
        att = ExitStack()
        late = ExitStack()
        ctx.enter_context(late)
        ctx.enter_context(att)
        x1 = sb("x1", [P, NT, D], F32, late)
        wo = sb("w_o", [P, DC, D], F32, late)
        gate = sb("gate", [P, DC, E], F32, late)
        sg_w, su_w = [sb(f"w_{n}", [P, DC, IS], F32, late) for n in ("sg", "su")]
        sd_w = sb("w_sd", [P, IS // P, D], F32, late)
        bo_b = sb("bo_b", [P, D], F32, late)
        half = sb("half", [P, QT], F32, late)
        xn = sb("xn", [P, QT, D], F32, late)
        xn2T = sb("xn2T", [P, DC, S], F32, late)
        stats = sb("stats", [P, QT, 6], F32, late)
        mv = sb("mv", [P, QT, 2], F32, late)
        rs = sb("rs", [P, 3, QT], F32, late)
        us = sb("us", [P, S], F32, late)
        rc = sb("rc", [P, QT, 4], F32, late)
        o_sb = sb("o_sb", [P, QT, D], F32, late)
        attnT = sb("attnT", [P, DC, S], F32, late)
        gel = sb("gel", [P, S], F32, late)
        hs = sb("hs", [P, IS // P, S], F32, late)
        ctx_sb = sb("ctx_sb", [P, DC, S], F32, att)
        negadj = sb("negadj", [P, QT, S], F32, att)
        am = [sb(f"am{i}", [P, QT, S], F32, att) for i in range(2)]
        wq, wk, wv = [sb(f"w_{n}", [P, DC, D], F32, att) for n in "qkv"]
        bqk = sb("bqk", [P, 2, DC], F32, att)
        bv_b = sb("bv_b", [P, D], F32, att)
        xlnT = sb("xlnT", [P, DC, S], F32, att)
        q32 = [sb(f"q32_{i}", [P, S], F32, att) for i in range(2)]
        parts = [sb(f"parts{i}", [P, 3, S], BF16, att) for i in range(2)]
        qs = [sb(f"qs{i}", [96, 4, S], BF16, att) for i in range(QK_RING)]
        ks = [sb(f"ks{i}", [96, 4, S], BF16, att) for i in range(QK_RING)]
        va = [sb(f"va{i}", [P, QT, H, 32], F32, att) for i in range(2)]
        sp_ = [sb(f"sp{i}", [P, S], F32, att) for i in range(8)]
        mn = sb("mn", [P, 8], F32, att)
        pt = [sb(f"pt{i}", [P, QT, S], F32, att) for i in range(PT_RING)]

        att.close()

        NSEG = NT // 2
        IC = I // P
        probs = sb("probs", [P, 2, NSEG, E], F32)
        soft = sb("soft", [P, NT, E], F32)
        soft1 = sb("soft1", [P, 3, NT], F32)
        ptok = sb("ptok", [P, 2 * P], F32)
        zeros = sb("zeros", [P, 2 * P], F32)
        above = sb("above", [P, 2 * P], F32)
        tied = sb("tied", [P, 2 * P], F32)
        prefix = sb("prefix", [P, 2 * P], F32)
        chosen = sb("chosen", [P, 2 * P], F32)
        same_e = sb("same_e", [P, P], F32)
        earlier = sb("earlier", [P, P], F32)
        bit = sb("bit", [P, 1], I32)
        theta = sb("theta", [P, 1], F32)
        cand = sb("cand", [P, 1], F32)
        cnt = sb("cnt", [P, 4], F32)
        slot_row = sb("slot_row", [P, C], BF16)
        slot_int = sb("slot_int", [P, C], I32)
        tok_int = sb("tok_int", [P, 2, NSEG, E], I32)
        rank = sb("rank", [P, NT, E], F32)
        route = sb("route", [P, NT, E, 5], BF16)
        rank_e = [sb(f"rank_e{i}", [P, NT, 1], F32) for i in range(2)]
        route_e = [sb(f"route_e{i}", [P, NT, 5], BF16) for i in range(2)]
        wres = sb("wres", [P, NT * E], F32)
        hot = [sb(f"hot{i}", [P, NT, C], BF16) for i in range(2)]
        rt = sb("rt", [P, 2, 5], F32)
        idx = [sb(f"idx{i}", [P, 2], U32) for i in range(2)]
        wt = [sb(f"wt{i}", [P, 2, 2], F32) for i in range(2)]
        xg = [sb(f"xg{i}", [P, 2, D], F32) for i in range(2)]
        xgT = [sb(f"xgT{i}", [P, DC, C], F32) for i in range(2)]
        wg_sb = [sb(f"wg{i}", [P, DC, I], F32) for i in range(2)]
        wu_sb = [sb(f"wu{i}", [P, DC, I], F32) for i in range(2)]
        wd_sb = [sb(f"wd{i}", [P, IC, D], F32) for i in range(2)]
        gl = [sb(f"gl{i}", [P, C], F32) for i in range(2)]
        hT = [sb(f"hT{i}", [P, IC, C], F32) for i in range(2)]
        eo = [sb(f"eo{i}", [P, 2, D], F32) for i in range(2)]

        s_top = sem("topk_chain")
        s_softin = sem("logits_shifted")
        s_softex = sem("logits_exp")
        s_probs = sem("probs_ready")
        s_ptokT = sem("probs_turned")
        s_cnt = sem("local_counts")
        s_tot = sem("total_counts")
        s_const = sem("topk_constants")
        s_pos = sem("slots_ready")
        s_posT = sem("slots_turned")
        s_route = sem("route_table")
        s_col = sem("expert_columns")
        s_hot = sem("one_hot_ready")
        s_ri = sem("routed")
        s_rt = sem("routes_chain")
        s_idx = sem("indices_ready")
        s_gath = [sem(f"gathered{i}") for i in range(2)]
        s_xgt = sem("gathered_turned")
        s_xgc = sem("gathered_copied")
        s_wgu = [sem(f"wgu_in{i}") for i in range(2)]
        s_wd = [sem(f"wd_in{i}") for i in range(2)]
        s_gu = sem("gate_up_ready")
        s_gl = sem("gelu_ready")
        s_h = sem("hidden_ready")
        s_dn = sem("down_ready")
        s_eo = sem("expert_out_ready")
        s_scat = sem("scattered")

        ps_i, ps_c, ps_d, ps_x = ps_s[0], ps_s[1], ps_m[0], ps_m[1]
        ps_g = [ps_t[0], ps_t[1], ps_u, ps_m[2]]

        def ps_g_of(k, i):
            return ps_g[(IC * k + i) % len(ps_g)]

        def experts(eng, body):
            for k in range(2):
                body(k, k, 0, False)
            with eng.Fori(1, E // 2 - 1) as p:
                for k in range(2):
                    body(2 * p + k, k, p, False)
            for k in range(2):
                body(E - 2 + k, k, E // 2 - 1, True)

        s_x = [sem(f"x_in{b}") for b in range(B)]
        s_cin = sem("ctx_in")
        s_mask = sem("mask_in")
        s_adj = sem("adj_in")
        s_w = sem("attn_weights_in")
        s_ws = sem("shared_weights_in")
        s_ident = sem("ident_ready")
        s_setup = sem("setup_done")
        s_pool = sem("pool_chain")
        s_dve = sem("dve_chain")
        s_stat = sem("stats_ready")
        s_rstd = sem("rstd_ready")
        s_xn = sem("normed_ready")
        s_am = sem("am_ready")
        s_xb = sem("x_plus_bias")
        s_parts = sem("parts_ready")
        s_stored = [sem(f"parts_stored{i}") for i in range(2)]
        s_qkin = [sem(f"qk_in{i}") for i in range(QK_RING)]
        s_score = sem("score_ready")
        s_added = sem("masked_scores_ready")
        s_exp = sem("exp_ready")
        s_tr = sem("transposes_ready")
        s_eva = sem("pt_by_act")
        s_evd = sem("pt_by_dve")
        s_pv = sem("pv_ready")
        s_us = sem("us_ready")
        s_m = sem("job_filled")
        s_done = {"act": sem("job_emptied_by_act"), "dve": sem("job_emptied_by_dve")}
        s_xst = sem("xn2_stored")
        s_out = sem("out_stored")

        def by_act(s):
            return s % 8 in (0, 2, 3, 5, 6)

        act_before = [0]
        for s in range(4, UNITS + 4):
            act_before.append(act_before[-1] + by_act(s))

        def wait_moved(eng, s):
            n = s - 4 + 1
            if act_before[n]:
                eng.wait_ge(s_eva, act_before[n])
            if n - act_before[n]:
                eng.wait_ge(s_evd, n - act_before[n])

        def wait_job(eng, *key):
            j = job[key]
            eng.wait_ge(s_done[j.engine], j.done)

        def bank(j):
            return ps_m[j.n % M_BANKS]

        block = ctx.enter_context(nc.Block())

        @block.sync
        def _(sp):
            def load_x(b):
                sp.dma_start(x1[:, QT * b:QT * b + QT, :], x_v[:, QT * b:QT * b + QT, :]).then_inc(s_x[b], 16)

            def load_ctx(b):
                if b:
                    wait_job(sp, "v", b - 1, 3)
                sp.dma_start(ctx_sb[:, :, :], ctxT.rearrange("(c p) t -> p c t", p=P)[:, :, S * b:S * b + S]).then_inc(s_cin, 16)

            def load_mask(b):
                if b >= 2:
                    sp.wait_ge(s_added, 64 * (b - 1))
                if b:
                    sp.wait_ge(s_am, b)
                sp.dma_start(am[b % 2][:, :, :].bitcast(I32), mask[b].rearrange("(n p) k -> p n k", p=P)).then_inc(s_mask, 16)

            def store_parts(b, k):
                n = 4 * b + k
                c, which = k // 2, k % 2
                sp.wait_ge(s_parts, n + 1)
                sp.dma_start(qk_d[b, which, :, P * c:P * c + P, :].rearrange("k f t -> f k t"), parts[n % 2][:, :, :]).then_inc(s_stored[n % 2], 16)

            def load_qk(G):
                b, g = G // 4, G % 4
                for i in range(2):
                    sp.wait_ge(s_stored[i], 32 * (b + 1))
                if G >= QK_RING:
                    sp.wait_ge(s_score, 16 * (G - QK_RING + 1))
                for which, (dst, kinds) in enumerate(((qs, Q_PART), (ks, K_PART))):
                    for i, kind in enumerate(kinds):
                        src = qk_d[b, which, kind, 64 * g:64 * g + 64, :].rearrange("(h d) t -> d h t", d=DH)
                        sp.dma_start(dst[G % QK_RING][16 * i:16 * i + 16, :, :], src).then_inc(s_qkin[G % QK_RING], 16)

            load_x(0)
            load_ctx(0)
            for t, src in ((wq, WqT), (wk, WkT), (wv, WvT)):
                sp.dma_start(t[:, :, :], src.rearrange("(c p) f -> p c f", p=P)).then_inc(s_w, 16)
            for i, src in enumerate((bq, bk)):
                sp.dma_start(bqk[:, i, :], src.rearrange("(c p) -> p c", p=P), allow_slow_non_contiguous=True).then_inc(s_w, 16)
            sp.dma_start(bv_b[:, :], bv.rearrange("(a f) -> a f", a=1).to_broadcast([P, D])).then_inc(s_w, 16)
            load_mask(0)
            sp.dma_start(negadj[:, :, :], adj.rearrange("(n p) k -> p n k", p=P)).then_inc(s_adj, 16)
            for s in range(FIRST, LAST):
                if s == -1:
                    for k in range(4):
                        store_parts(0, k)
                    for G in range(QK_RING):
                        load_qk(G)
                    sp.dma_start(bo_b[:, :], bo.rearrange("(a f) -> a f", a=1).to_broadcast([P, D])).then_inc(s_ws, 16)
                    sp.dma_start(wo[:, :, :], WoT.rearrange("(c p) f -> p c f", p=P)).then_inc(s_ws, 16)
                    for b in range(1, B):
                        load_x(b)
                    for t, src in ((gate, gateT), (sg_w, SgT), (su_w, SuT), (sd_w, SdT)):
                        sp.dma_start(t[:, :, :], src.rearrange("(c p) f -> p c f", p=P)).then_inc(s_ws, 16)
                b, r = s // 64 + 1, s % 64
                if 0 < b < B:
                    if r == 0:
                        load_ctx(b)
                    if r == 2:
                        load_mask(b)
                    if r in (16, 20, 24, 28):
                        store_parts(b, (r - 16) // 4)
                if (s + 28) % 16 == 0 and QK_RING <= (s + 28) // 16 < 4 * B:
                    load_qk((s + 28) // 16)
                b = s // 64 - 1
                if b >= 0 and s % 64 == 24:
                    sp.wait_ge(s_xn, norm_n[2, b] + 1)
                    sp.dma_start(xn2_d.rearrange("(n p) d -> p n d", p=P)[:, QT * b:QT * b + QT, :], xn[:, :, :]).then_inc(s_xst, 16)
                if b >= 0 and s % 64 == 62:
                    wait_job(sp, "dn", b, 3)
                    sp.dma_start(out_v[:, QT * b:QT * b + QT, :], x1[:, QT * b:QT * b + QT, :]).then_inc(s_out, 16)
            sp.wait_ge(s_xst, 16 * B)

            def load_up(e, k):
                for t, src in ((wg_sb, WgT), (wu_sb, WuT)):
                    sp.dma_start(t[k][:, :, :], src[bass.ds(e, 1)].rearrange("a (c p) i -> p (a c) i", p=P)).then_inc(s_wgu[k], 16)

            def load_down(e, k):
                sp.dma_start(wd_sb[k][:, :, :], WdT[bass.ds(e, 1)].rearrange("a (c p) d -> p (a c) d", p=P)).then_inc(s_wd[k], 16)

            def body(e, k, p, last):
                if not last:
                    sp.wait_ge(s_gu, IC * e + IC)
                    load_up(e + 2, k)
                    sp.wait_ge(s_dn, e + 1)
                    load_down(e + 2, k)

            sp.wait_ge(s_us, 4 * B)
            for k in range(2):
                load_up(k, k)
                load_down(k, k)
            experts(sp, body)

        @block.gpsimd
        def _(pool):
            chain = [0]

            def link(ins):
                chain[0] += 1
                ins.then_inc(s_pool, 1)
                pool.wait_ge(s_pool, chain[0])

            link(pool.memset(ident[:, :], 0.0))
            pool.affine_select(out=ident[:, :], in_=ident[:, :], compare_op=ALU.not_equal, fill=1.0,
                               base=0, pattern=[[-1, P]], channel_multiplier=1).then_inc(s_ident, 1)
            pool.memset(half[:, :], -0.5).then_inc(s_setup, 1)
            for i in range(2):
                link(pool.memset(va[i][:, :, :, DH:32], 0.0))
                pool.memset(va[i][:, :, :, DH:DH + 1], 1.0).then_inc(s_setup, 1)
            pool.wait_ge(s_setup, 3)

            def rstd(n):
                pool.wait_ge(s_stat, n + 1)
                link(pool.tensor_scalar(rs[:, 1, :], mv[:, :, 1], EPS, None, ALU.add))
                link(pool.tensor_tensor(rs[:, 0, :], rs[:, 1, :], half[:, :], ALU.pow))
                link(pool.tensor_tensor(rs[:, 2, :], rs[:, 0, :], rs[:, 0, :], ALU.mult))
                link(pool.tensor_tensor(rs[:, 2, :], rs[:, 2, :], rs[:, 1, :], ALU.mult))
                link(pool.tensor_scalar(rs[:, 2, :], rs[:, 2, :], -0.5, 1.5, ALU.mult, ALU.add))
                pool.tensor_tensor(rs[:, 0, :], rs[:, 0, :], rs[:, 2, :], ALU.mult).then_inc(s_rstd, 1)

            def split(b, k):
                n = 4 * b + k
                wait_job(pool, "qk"[k % 2], b, k // 2)
                if n >= 2:
                    pool.wait_ge(s_stored[n % 2], 16 * (n // 2))
                q, p = q32[n % 2], parts[n % 2]
                link(pool.tensor_copy(p[:, 0, :], q[:, :]))
                link(pool.tensor_tensor(q[:, :], q[:, :], p[:, 0, :], ALU.subtract))
                link(pool.tensor_copy(p[:, 1, :], q[:, :]))
                pool.tensor_tensor(p[:, 2, :], q[:, :], p[:, 1, :], ALU.subtract).then_inc(s_parts, 1)

            def build_am(b):
                pool.wait_ge(s_mask, 16 * (b + 1))
                if b == 0:
                    pool.wait_ge(s_adj, 16)
                a = am[b % 2]
                link(pool.tensor_scalar(a[:, :, :], a[:, :, :].bitcast(I32), 0.0, MASKED, ALU.is_equal, ALU.mult))
                pool.tensor_tensor(a[:, :, :], a[:, :, :], negadj[:, :, :], ALU.subtract).then_inc(s_am, 1)

            def add_bias(b):
                if b == 0:
                    pool.wait_ge(s_ws, 16 * 6)
                pool.wait_ge(s_xn, norm_n[1, b] + 1)
                for t in range(QT * b, QT * b + QT):
                    i = pool.tensor_tensor(x1[:, t, :], x1[:, t, :], bo_b[:, :], ALU.add)
                i.then_inc(s_xb, 1)

            for s in range(FIRST, LAST):
                for n, (at, which, b) in enumerate(norms):
                    if at == s:
                        rstd(n)
                b, r = s // 64 + 1, s % 64
                if s == -1:
                    for k in range(4):
                        split(0, k)
                    build_am(0)
                    add_bias(0)
                if 0 < b < B:
                    if r in (14, 18, 22, 26):
                        split(b, (r - 14) // 4)
                    if r == 30:
                        build_am(b)
                    if r == 33:
                        add_bias(b)

            pool.wait_ge(s_us, 4 * B)
            link(pool.iota(tok_int[:, :, :, :], [[P, 2], [2 * P, NSEG], [0, E]], base=0, channel_multiplier=0))
            link(pool.tensor_copy(route[:, :, :, 0], tok_int[:, :, :, :].rearrange("p h s e -> p (h s) e")))
            link(pool.iota(tok_int[:, :, :, :], [[0, 2], [0, NSEG], [0, E]], base=0, channel_multiplier=1))
            link(pool.tensor_copy(route[:, :, :, 1], tok_int[:, :, :, :].rearrange("p h s e -> p (h s) e")))
            link(pool.iota(slot_int[:, :], [[1, C]], base=1, channel_multiplier=0))
            link(pool.tensor_copy(slot_row[:, :], slot_int[:, :]))
            link(pool.memset(same_e[:, :], 0.0))
            for m in range(1 - NSEG, NSEG):
                link(pool.affine_select(out=same_e[:, :], in_=same_e[:, :], compare_op=ALU.not_equal, fill=1.0,
                                        base=-E * m, pattern=[[-1, P]], channel_multiplier=1))
            link(pool.affine_select(out=earlier[:, :], in_=same_e[:, :], compare_op=ALU.is_gt, fill=0.0,
                                    base=0, pattern=[[1, P]], channel_multiplier=-1))
            pool.memset(zeros[:, :], 0.0).then_inc(s_const, 1)

            def gather(e, k, p):
                pool.wait_ge(s_idx, e + 1)
                pool.wait_ge(s_xst, 16 * B)
                for ch in range(2):
                    pool.indirect_dma_start(out=xg[k][:, ch, :], out_offset=None, in_=xn2_d,
                                            in_offset=bass.IndirectOffsetOnAxis(ap=idx[k][:, ch:ch + 1], axis=0)).then_inc(s_gath[k], 16)

            def scatter(e, k):
                pool.wait_ge(s_eo, e + 1)
                if not isinstance(e, int) or e:
                    pool.wait_ge(s_scat, 32 * e)
                pool.wait_ge(s_out, 16 * B)
                for ch in range(2):
                    pool.indirect_dma_start(out=out, out_offset=bass.IndirectOffsetOnAxis(ap=idx[k][:, ch:ch + 1], axis=0),
                                            in_=eo[k][:, ch, :], in_offset=None,
                                            compute_op=ALU.add).then_inc(s_scat, 16)

            def body(e, k, p, last):
                if not (last and k == 1):
                    gather(e + 1, 1 - k, p + k)
                scatter(e, k)

            gather(0, 0, 0)
            for e in range(E):
                body(e, e % 2, e // 2, e == E - 1)
            pool.wait_ge(s_scat, 32 * E)

        @block.scalar
        def _(act):
            def exp(u):
                act.wait_ge(s_added, u + 1)
                act.activation(sp_[u % 8][:, :], sp_[u % 8][:, :], ACT.Exp, bias=mn[:, u % 8:u % 8 + 1], scale=-1.0).then_inc(s_exp, 1)

            def move_pt(s):
                h, kt = s // 4 - 1, s % 4
                act.wait_ge(s_tr, s - 4 + 1)
                if h >= PT_RING:
                    act.wait_ge(s_pv, 4 * ((h - PT_RING) // 4 + 1))
                act.activation(pt[h % PT_RING][:, kt, :], ps_t[s % 2][:, :], ACT.Copy).then_inc(s_eva, 1)

            def empty(j):
                act.wait_ge(s_m, j.n + 1)
                m = bank(j)
                if j.kind == "xT":
                    if j.b:
                        wait_job(act, "k", j.b - 1, 1)
                    i = act.activation(xlnT[:, j.i, :], m[:, :], ACT.Copy)
                if j.kind == "aT":
                    if j.b:
                        wait_job(act, "y", j.b - 1, 3)
                    i = act.activation(attnT[:, j.i, :], m[:, :], ACT.Copy)
                if j.kind == "xn2T":
                    if j.b:
                        wait_job(act, "su", j.b - 1, 3)
                    i = act.activation(xn2T[:, j.i, :], m[:, :], ACT.Copy)
                if j.kind == "sg":
                    if j.b or j.i:
                        wait_job(act, "su", j.b if j.i else j.b - 1, (j.i + 3) % 4)
                    i = act.activation(gel[:, :], m[:, :], ACT.Gelu)
                i.then_inc(s_done["act"], 1)

            for s in range(FIRST, LAST):
                if 0 <= s - 1 < UNITS:
                    exp(s - 1)
                if 4 <= s - 1 < UNITS + 4 and by_act(s - 1):
                    move_pt(s - 1)
                G = s // 16 - 1
                if s % 16 == 8 and 0 <= G < 4 * B:
                    act.wait_ge(s_pv, 4 * (G + 1))
                    if G:
                        act.wait_ge(s_m, job["norm", (G - 1) // 4, (G - 1) % 4].n + 1)
                    act.activation(us[:, :], ps_u[:, :], ACT.Copy).then_inc(s_us, 1)
                for j in jobs:
                    if j.step == s - 1 and j.engine == "act":
                        empty(j)

            act.wait_ge(s_softin, 1)
            act.activation(soft[:, :, :], soft[:, :, :], ACT.Exp).then_inc(s_softex, 1)

            def copy_gathered(e, k):
                act.wait_ge(s_xgt, e + 1)
                act.activation(xgT[k][:, :, :], ps_x[:, :].rearrange("p (c t) -> p c t", c=DC), ACT.Copy).then_inc(s_xgc, 1)

            def body(e, k, p, last):
                for i in range(IC):
                    act.wait_ge(s_gu, IC * e + i + 1)
                    if not isinstance(p, int) or p or k or i >= 2:
                        act.wait_ge(s_h, IC * e + i - 1)
                    act.activation(gl[i % 2][:, :], ps_g_of(k, i)[:, 0:C], ACT.Gelu).then_inc(s_gl, 1)
                if not (last and k == 1):
                    copy_gathered(e + 1, 1 - k)

            copy_gathered(0, 0)
            experts(act, body)

        @block.vector
        def _(dve):
            chain = [0]

            def link(ins):
                chain[0] += 1
                ins.then_inc(s_dve, 1)
                dve.wait_ge(s_dve, chain[0])

            def add_mask(u):
                b, qt = u // 64, u % 4
                dve.wait_ge(s_score, u + 1)
                if u % 64 == 0:
                    dve.wait_ge(s_am, b + 1)
                if u >= 8:
                    dve.wait_ge(s_tr, 4 * (u // 4 - 1))
                dve.tensor_tensor_reduce(sp_[u % 8][:, :], ps_s[u % 2][:, :], am[b % 2][:, qt, :], 1.0, LARGEST,
                                         ALU.add, ALU.min, mn[:, u % 8:u % 8 + 1]).then_inc(s_added, 1)

            def move_pt(s):
                h, kt = s // 4 - 1, s % 4
                dve.wait_ge(s_tr, s - 4 + 1)
                if h >= PT_RING:
                    dve.wait_ge(s_pv, 4 * ((h - PT_RING) // 4 + 1))
                dve.tensor_copy(pt[h % PT_RING][:, kt, :], ps_t[s % 2][:, :]).then_inc(s_evd, 1)

            def statistics(n, b):
                if n:
                    dve.wait_ge(s_xn, n)
                for t in range(QT):
                    i = dve.bn_stats(stats[:, t, :], x1[:, QT * b + t, :])
                link(i)
                for t in range(QT):
                    i = dve.bn_aggr(mv[:, t, :], stats[:, t, :])
                i.then_inc(s_stat, 1)

            def apply(n, which, b):
                dve.wait_ge(s_rstd, n + 1)
                if n:
                    _, w, pb = norms[n - 1]
                    dve.wait_ge(s_m, job["xT" if w == 1 else "xn2T", pb, 1].n + 1)
                    stored = sum(1 for _, w, _ in norms[:n] if w == 2)
                    if stored:
                        dve.wait_ge(s_xst, 16 * stored)
                for t in range(QT):
                    i = dve.tensor_scalar(xn[:, t, :], x1[:, QT * b + t, :], mv[:, t, 0:1], rs[:, 0, t:t + 1],
                                          ALU.subtract, ALU.mult)
                i.then_inc(s_xn, 1)

            def empty(j):
                dve.wait_ge(s_m, j.n + 1)
                m, b, i = bank(j), j.b, j.i
                if j.kind in "qk":
                    k = 2 * i + (j.kind == "k")
                    n = 4 * b + k
                    if n >= 2:
                        dve.wait_ge(s_parts, n - 1)
                    which = int(j.kind == "k")
                    scale = -1.0 / DH ** 0.5 if j.kind == "q" else 1.0
                    last = dve.tensor_scalar(q32[n % 2][:, :], m[:, :], bqk[:, which, i:i + 1], scale, ALU.add, ALU.mult)
                if j.kind == "v":
                    if b >= 2:
                        dve.wait_ge(s_pv, 16 * (b - 1))
                    last = dve.tensor_tensor(va[b % 2][:, i, :, 0:DH], m[:, 0:D].rearrange("p (h d) -> p h d", h=H),
                                             bv_b[:, :].rearrange("p (h d) -> p h d", h=H), ALU.add)
                if j.kind == "norm":
                    mm = m[:, :].rearrange("p (q j r) -> p q j r", q=QT, r=32)
                    if b and i == 0:
                        dve.wait_ge(s_m, job["aT", b - 1, 1].n + 1)
                    link(dve.reciprocal(rc[:, :, :], mm[:, :, :, DH]))
                    last = dve.tensor_tensor(o_sb[:, :, 64 * i:64 * i + 64].rearrange("p q (j d) -> p q j d", d=DH),
                                             mm[:, :, :, 0:DH], rc[:, :, :].unsqueeze(3).to_broadcast([P, QT, 4, DH]), ALU.mult)
                if j.kind == "y":
                    if i == 0:
                        dve.wait_ge(s_xb, b + 1)
                    last = dve.tensor_tensor(x1[:, QT * b + i, :], m[:, 0:D], x1[:, QT * b + i, :], ALU.add)
                if j.kind == "lg":
                    last = dve.tensor_copy(logits[:, QT * b:QT * b + QT, :], m[:, 0:QT * E].rearrange("p (q e) -> p q e", e=E))
                if j.kind == "su":
                    wait_job(dve, "sg", b, i)
                    if b and i == 0:
                        dve.wait_ge(s_m, job["dn", b - 1, 3].n + 1)
                    last = dve.tensor_tensor(hs[:, i, :], m[:, :], gel[:, :], ALU.mult)
                if j.kind == "dn":
                    last = dve.tensor_tensor(x1[:, QT * b + i, :], m[:, 0:D], x1[:, QT * b + i, :], ALU.add)
                last.then_inc(s_done["dve"], 1)

            for b in range(B):
                pass
            for s in range(FIRST, LAST):
                if s == -14:
                    dve.wait_ge(s_w, 16 * 6)
                    dve.wait_ge(s_setup, 3)
                if 0 <= s < UNITS:
                    add_mask(s)
                if 4 <= s - 1 < UNITS + 4 and not by_act(s - 1):
                    move_pt(s - 1)
                for n, (at, which, b) in enumerate(norms):
                    if at == s:
                        if which == 1:
                            dve.wait_ge(s_x[b], 16)
                        else:
                            wait_job(dve, "y", b, 3)
                        statistics(n, b)
                    if at + 2 == s:
                        apply(n, which, b)
                for j in jobs:
                    if j.step == s - 1 and j.engine == "dve":
                        empty(j)

            top = [0]

            def then(ins):
                top[0] += 1
                ins.then_inc(s_top, 1)
                dve.wait_ge(s_top, top[0])

            dve.wait_ge(s_us, 4 * B)
            then(dve.tensor_reduce(soft1[:, 0, :], logits[:, :, :], AX.X, ALU.max))
            dve.tensor_tensor(soft[:, :, :], logits[:, :, :], soft1[:, 0, :].unsqueeze(2).to_broadcast([P, NT, E]), ALU.subtract).then_inc(s_softin, 1)
            dve.wait_ge(s_softex, 1)
            then(dve.tensor_reduce(soft1[:, 1, :], soft[:, :, :], AX.X, ALU.add))
            then(dve.reciprocal(soft1[:, 2, :], soft1[:, 1, :]))
            dve.tensor_tensor(probs[:, :, :, :], soft[:, :, :].rearrange("p (s h) e -> p h s e", h=2),
                              soft1[:, 2, :].rearrange("p (s h) -> p h s", h=2).unsqueeze(3).to_broadcast([P, 2, NSEG, E]), ALU.mult).then_inc(s_probs, 1)
            dve.wait_ge(s_probs, 1)
            flat = probs[:, :, :, :].rearrange("p h s e -> p (h s e)")
            flat_route = route[:, :, :, :].rearrange("p n e k -> p (n e) k")
            dve.wait_ge(s_const, 1)
            then(dve.tensor_copy(flat_route[:, :, 2], flat))
            then(dve.tensor_tensor(wres[:, :], flat, flat_route[:, :, 2], ALU.subtract))
            then(dve.tensor_copy(flat_route[:, :, 3], wres[:, :]))
            dve.tensor_tensor(flat_route[:, :, 4], wres[:, :], flat_route[:, :, 3], ALU.subtract).then_inc(s_route, 1)

            then(dve.memset(bit[:, :], 1 << 29))
            then(dve.memset(theta[:, :], 0.0))
            dve.wait_ge(s_ptokT, 1)
            then(dve.tensor_copy(ptok[:, :], ps_i[:, 0:2 * P]))
            ROUNDS = 30
            with dve.Fori(0, ROUNDS) as n:
                STEPS = 4
                at = top[0] + STEPS * n
                dve.tensor_tensor(cand[:, :].bitcast(I32), theta[:, :].bitcast(I32), bit[:, :], ALU.bitwise_or).then_inc(s_top, 1)
                dve.wait_ge(s_top, at + 1)
                dve.tensor_scalar(prefix[:, :], ptok[:, :], cand[:, 0:1], 0.0, ALU.is_ge, ALU.add, accum_out=cnt[:, 0:1]).then_inc(s_cnt, 1)
                dve.tensor_scalar(bit[:, :], bit[:, :], 1, None, ALU.logical_shift_right).then_inc(s_top, 1)
                dve.wait_ge(s_tot, n + 1)
                dve.tensor_scalar(cnt[:, 1:2], ps_c[:, 0:1], float(C), cand[:, 0:1], ALU.is_ge, ALU.mult).then_inc(s_top, 1)
                dve.wait_ge(s_top, at + 3)
                dve.tensor_tensor(theta[:, :], theta[:, :], cnt[:, 1:2], ALU.max).then_inc(s_top, 1)
                dve.wait_ge(s_top, at + 4)
            top[0] += STEPS * ROUNDS
            then(dve.tensor_scalar(above[:, :], ptok[:, :], theta[:, 0:1], 0.0, ALU.is_gt, ALU.add, accum_out=cnt[:, 0:1]))
            then(dve.tensor_scalar(tied[:, :], ptok[:, :], theta[:, 0:1], 0.0, ALU.is_equal, ALU.add, accum_out=cnt[:, 1:2]))
            dve.tensor_tensor_scan(prefix[:, :], tied[:, :], zeros[:, :], 0.0, ALU.add, ALU.add).then_inc(s_cnt, 1)
            dve.wait_ge(s_tot, ROUNDS + 1)
            then(dve.tensor_copy(cnt[:, 2:4], ps_c[:, 0:2]))
            then(dve.tensor_tensor(cnt[:, 2:3], cnt[:, 2:3], cnt[:, 3:4], ALU.add))
            then(dve.tensor_scalar(cnt[:, 2:3], cnt[:, 2:3], -1.0, float(C), ALU.mult, ALU.add))
            dve.wait_ge(s_cnt, ROUNDS + 1)
            then(dve.scalar_tensor_tensor(tied[:, :], prefix[:, :], cnt[:, 2:3], tied[:, :], ALU.is_le, ALU.mult))
            dve.scalar_tensor_tensor(chosen[:, :], tied[:, :], 1.0, above[:, :], ALU.mult, ALU.add, accum_out=cnt[:, 0:1]).then_inc(s_cnt, 1)
            dve.wait_ge(s_cnt, ROUNDS + 2)
            then(dve.tensor_tensor_scan(prefix[:, :], chosen[:, :], zeros[:, :], 0.0, ALU.add, ALU.add))
            dve.wait_ge(s_tot, ROUNDS + 2)
            dve.scalar_tensor_tensor(prefix[:, :], prefix[:, :], ps_c[:, 0:1], chosen[:, :], ALU.add, ALU.mult).then_inc(s_pos, 1)
            dve.wait_ge(s_posT, 1)
            then(dve.tensor_copy(rank[:, :, :], ps_i[:, 0:2 * P].rearrange("p (n e) -> p n e", e=E)))

            def one_hot(e, k):
                if not isinstance(e, int) or e >= 2:
                    dve.wait_ge(s_ri, e - 1)
                dve.tensor_copy(rank_e[k][:, :, :], rank[:, :, bass.ds(e, 1)]).then_inc(s_col, 1)
                dve.tensor_copy(route_e[k][:, :, :], route[:, :, bass.ds(e, 1), :].rearrange("p n a k -> p n (a k)"))
                dve.wait_ge(s_col, e + 1)
                for n in range(NT):
                    i = dve.tensor_scalar(hot[k][:, n, :], slot_row[:, :], rank_e[k][:, n, :], None, ALU.is_equal)
                i.then_inc(s_hot, 1)

            def take_routes(e, k):
                dve.wait_ge(s_ri, e + 1)
                r = ps_i[:, 0:10].rearrange("p (c k) -> p c k", k=5)
                if not isinstance(e, int) or e >= 2:
                    dve.wait_ge(s_scat, 32 * (e - 1))
                dve.tensor_copy(rt[:, :, :], r).then_inc(s_rt, 1)
                dve.wait_ge(s_rt, 2 * e + 1)
                dve.tensor_tensor(idx[k][:, :], rt[:, :, 0], rt[:, :, 1], ALU.add)
                dve.tensor_tensor(wt[k][:, 0, :], rt[:, :, 2], rt[:, :, 3], ALU.add).then_inc(s_rt, 1)
                dve.wait_ge(s_rt, 2 * e + 2)
                dve.tensor_tensor(wt[k][:, 1, :], wt[k][:, 0, :], rt[:, :, 4], ALU.add).then_inc(s_idx, 1)

            def body(e, k, p, last):
                if not (last and k == 1):
                    one_hot(e + 1, 1 - k)
                for i in range(IC):
                    if i == 2 and not (last and k == 1):
                        take_routes(e + 1, 1 - k)
                    dve.wait_ge(s_gl, IC * e + i + 1)
                    if i == 0 and (not isinstance(p, int) or p):
                        dve.wait_ge(s_dn, e - 1)
                    dve.tensor_tensor(hT[k][:, i, :], ps_g_of(k, i)[:, C:2 * C], gl[i % 2][:, :], ALU.mult).then_inc(s_h, 1)
                dve.wait_ge(s_dn, e + 1)
                dve.wait_ge(s_idx, e + 1)
                for ch in range(2):
                    i = dve.tensor_scalar(eo[k][:, ch, :], ps_d[:, D * ch:D * ch + D], wt[k][:, 1, ch:ch + 1], None, ALU.mult)
                i.then_inc(s_eo, 1)

            one_hot(0, 0)
            take_routes(0, 0)
            experts(dve, body)

        @block.tensor
        def _(pe):
            def score(u):
                G, h, qt = u // 16, (u // 4) % 4, u % 4
                if u % 16 == 0:
                    pe.wait_ge(s_qkin[G % QK_RING], 16 * 12 * (G // QK_RING + 1))
                if u >= 2:
                    pe.wait_ge(s_added, u - 1)
                pe.matmul(ps_s[u % 2][:, :], qs[G % QK_RING][:, h, P * qt:P * qt + P], ks[G % QK_RING][:, h, :],
                          start=True, stop=True).then_inc(s_score, 1)

            def transposes(s):
                h, kt = s // 4 - 1, s % 4
                if kt == 0:
                    pe.wait_ge(s_exp, 4 * h + 4)
                if s - 2 >= 4:
                    wait_moved(pe, s - 2)
                for qt in range(QT):
                    i = pe.transpose(ps_t[s % 2][:, P * qt:P * qt + P], sp_[(4 * h + qt) % 8][:, P * kt:P * kt + P], ident[:, :])
                i.then_inc(s_tr, 1)

            def pv(G, kt):
                if kt == 0 and G:
                    pe.wait_ge(s_us, G)
                wait_moved(pe, 16 * (G + 1) + kt)
                b, g = G // 4, G % 4
                for j in range(4):
                    i = pe.matmul(ps_u[32 * j:32 * j + 32, :], va[b % 2][:, kt, 4 * g + j, :], pt[(4 * G + j) % PT_RING][:, kt, :],
                                  start=(kt == 0), stop=(kt == 3))
                i.then_inc(s_pv, 1)

            def fill(j):
                m, b, i = bank(j), j.b, j.i
                if j.n >= M_BANKS:
                    e = jobs[j.n - M_BANKS]
                    pe.wait_ge(s_done[e.engine], e.done)
                if j.kind in ("xT", "xn2T"):
                    pe.wait_ge(s_xn, norm_n[1 if j.kind == "xT" else 2, b] + 1)
                    for t in range(QT):
                        last = pe.transpose(m[:, P * t:P * t + P], xn[:, t, P * i:P * i + P], ident[:, :])
                if j.kind in "qk":
                    wait_job(pe, "xT", b, 1)
                    pe.wait_ge(s_cin, 16 * (b + 1))
                    if b == 0 and i == 0:
                        pe.wait_ge(s_w, 16 * 6)
                    w, src = (wq, xlnT) if j.kind == "q" else (wk, ctx_sb)
                    for c in range(DC):
                        last = pe.matmul(m[:, :], w[:, c, P * i:P * i + P], src[:, c, :], start=(c == 0), stop=(c == DC - 1))
                if j.kind == "v":
                    for c in range(DC):
                        last = pe.matmul(m[:, 0:D], ctx_sb[:, c, P * i:P * i + P], wv[:, c, :], start=(c == 0), stop=(c == DC - 1))
                if j.kind == "norm":
                    pe.wait_ge(s_us, 4 * b + i + 1)
                    for t in range(QT):
                        last = pe.transpose(m[:, P * t:P * t + P], us[:, P * t:P * t + P], ident[:, :])
                if j.kind == "aT":
                    wait_job(pe, "norm", b, 3)
                    for t in range(QT):
                        last = pe.transpose(m[:, P * t:P * t + P], o_sb[:, t, P * i:P * i + P], ident[:, :])
                if j.kind == "y":
                    wait_job(pe, "aT", b, 1)
                    if b == 0 and i == 0:
                        pe.wait_ge(s_ws, 16 * 6)
                    for c in range(DC):
                        last = pe.matmul(m[:, 0:D], attnT[:, c, P * i:P * i + P], wo[:, c, :], start=(c == 0), stop=(c == DC - 1))
                if j.kind == "lg":
                    wait_job(pe, "xn2T", b, 1)
                    for t in range(QT):
                        for c in range(DC):
                            last = pe.matmul(m[:, E * t:E * t + E], xn2T[:, c, P * t:P * t + P], gate[:, c, :], start=(c == 0), stop=(c == DC - 1))
                if j.kind in ("sg", "su"):
                    wait_job(pe, "xn2T", b, 1)
                    w = sg_w if j.kind == "sg" else su_w
                    for c in range(DC):
                        last = pe.matmul(m[:, :], w[:, c, P * i:P * i + P], xn2T[:, c, :], start=(c == 0), stop=(c == DC - 1))
                if j.kind == "dn":
                    wait_job(pe, "su", b, 3)
                    for c in range(IS // P):
                        last = pe.matmul(m[:, 0:D], hs[:, c, P * i:P * i + P], sd_w[:, c, :], start=(c == 0), stop=(c == IS // P - 1))
                last.then_inc(s_m, 1)

            pe.wait_ge(s_ident, 1)
            for s in range(FIRST, LAST):
                if s == 0:
                    pe.wait_ge(s_setup, 3)
                if 0 <= s < UNITS:
                    score(s)
                if 4 <= s < UNITS + 4:
                    transposes(s)
                G = s // 16 - 1
                if 0 <= G < 4 * B and 4 <= s % 16 < 8:
                    pv(G, s % 16 - 4)
                for j in jobs:
                    if j.step == s:
                        fill(j)

            pe.wait_ge(s_probs, 1)
            for hf in range(2):
                i = pe.transpose(ps_i[:, P * hf:P * hf + P], probs[:, hf, :, :].rearrange("p s e -> p (s e)"), ident[:, :])
            i.then_inc(s_ptokT, 1)
            pe.wait_ge(s_const, 1)
            ROUNDS = 30
            with pe.Fori(0, ROUNDS) as n:
                pe.wait_ge(s_cnt, n + 1)
                pe.matmul(ps_c[:, 0:1], same_e[:, :], cnt[:, 0:1], start=True, stop=True).then_inc(s_tot, 1)
            pe.wait_ge(s_cnt, ROUNDS + 1)
            pe.matmul(ps_c[:, 0:1], same_e[:, :], cnt[:, 0:1], start=True, stop=True)
            pe.matmul(ps_c[:, 1:2], earlier[:, :], cnt[:, 1:2], start=True, stop=True).then_inc(s_tot, 1)
            pe.wait_ge(s_cnt, ROUNDS + 2)
            pe.matmul(ps_c[:, 0:1], earlier[:, :], cnt[:, 0:1], start=True, stop=True).then_inc(s_tot, 1)
            pe.wait_ge(s_pos, 1)
            for hf in range(2):
                i = pe.transpose(ps_i[:, P * hf:P * hf + P], prefix[:, P * hf:P * hf + P], ident[:, :])
            i.then_inc(s_posT, 1)
            pe.wait_ge(s_route, 1)

            def routes(e, k):
                pe.wait_ge(s_hot, e + 1)
                if not isinstance(e, int) or e:
                    pe.wait_ge(s_idx, e)
                for ch in range(2):
                    for n in range(NT):
                        i = pe.matmul(ps_i[:, 5 * ch:5 * ch + 5], hot[k][:, n, P * ch:P * ch + P], route_e[k][:, n, :],
                                      start=(n == 0), stop=(n == NT - 1))
                i.then_inc(s_ri, 1)

            def turn_gathered(e, k, p):
                pe.wait_ge(s_gath[k], 32 * (p + 1))
                if not isinstance(e, int) or e:
                    pe.wait_ge(s_xgc, e)
                for c in range(DC):
                    for ch in range(2):
                        i = pe.transpose(ps_x[:, C * c + P * ch:C * c + P * ch + P], xg[k][:, ch, P * c:P * c + P], ident[:, :])
                i.then_inc(s_xgt, 1)

            def body(e, k, p, last):
                pe.wait_ge(s_xgc, e + 1)
                pe.wait_ge(s_wgu[k], 32 * (p + 1))
                for i in range(IC):
                    if i == 2 and not (last and k == 1):
                        routes(e + 1, 1 - k)
                    if not isinstance(p, int) or p or k or i >= len(ps_g):
                        pe.wait_ge(s_h, IC * e + i - len(ps_g) + 1)
                    for which, w in enumerate((wg_sb, wu_sb)):
                        for c in range(DC):
                            m = pe.matmul(ps_g_of(k, i)[:, C * which:C * which + C], w[k][:, c, P * i:P * i + P], xgT[k][:, c, :],
                                          start=(c == 0), stop=(c == DC - 1))
                    m.then_inc(s_gu, 1)
                if not (last and k == 1):
                    turn_gathered(e + 1, 1 - k, p + k)
                pe.wait_ge(s_wd[k], 16 * (p + 1))
                pe.wait_ge(s_h, IC * e + IC)
                if not isinstance(p, int) or p or k:
                    pe.wait_ge(s_eo, e)
                for ch in range(2):
                    for i in range(IC):
                        m = pe.matmul(ps_d[:, D * ch:D * ch + D], hT[k][:, i, P * ch:P * ch + P], wd_sb[k][:, i, :],
                                      start=(i == 0), stop=(i == IC - 1))
                m.then_inc(s_dn, 1)

            routes(0, 0)
            turn_gathered(0, 0, 0)
            experts(pe, body)


_OUTS = [((4, 512, 256), "float32")]


def kernel(**inputs):
    import numpy as _np
    import concourse.bacc as _bacc
    from concourse import mybir as _mybir
    from concourse.bass_utils import run_bass_kernel_spmd as _run

    a = {k: _np.asarray(v) for k, v in inputs.items()}
    p = {k[len("L0_xattn_"):]: v for k, v in a.items() if k.startswith("L0_xattn_")}
    f = {k[len("L0_ffn_"):]: v for k, v in a.items() if k.startswith("L0_ffn_")}
    x = a["x"]
    d = x.shape[-1]
    arrays = {
        "x": x.reshape(-1, d), "ctxT": a["ctx_1024"].reshape(-1, d).T, "mask": a["mask_Bx1xSxS2_ik1"][:, 0],
        "adj": p["adj"], "WqT": p["Wq"].T, "bq": p["bq"], "WkT": p["Wk"].T, "bk": p["bk"],
        "WvT": p["Wv"].T, "bv": p["bv"], "WoT": p["Wo"].T, "bo": p["bo"], "gateT": f["gate_w"].T,
        "WgT": f["Wg"].transpose(0, 2, 1), "WuT": f["Wu"].transpose(0, 2, 1), "WdT": f["Wd"].transpose(0, 2, 1),
        "SgT": f["Sg"].T, "SuT": f["Su"].T, "SdT": f["Sd"].T,
    }
    arrays = {k: _np.ascontiguousarray(v) for k, v in arrays.items()}
    nc = _bacc.Bacc("TRN2", target_bir_lowering=False, num_devices=1)
    args = [nc.dram_tensor(f"in_{k}", v.shape, _mybir.dt.from_np(v.dtype), kind="ExternalInput").ap()
            for k, v in arrays.items()]
    out = nc.dram_tensor("out_0", [x.shape[0] * x.shape[1], d], F32, kind="ExternalOutput").ap()
    build(nc, *args, out)
    r = _run(nc, [{f"in_{k}": v for k, v in arrays.items()}], core_ids=[0])
    return r.results[0]["out_0"].reshape(x.shape)
```

```python
from contextlib import ExitStack

import concourse.bass as bass
from concourse import mybir

ALU = mybir.AluOpType
ACT = mybir.ActivationFunctionType
F32 = mybir.dt.float32
F32R = mybir.dt.float32r
BF16 = mybir.dt.bfloat16
I32 = mybir.dt.int32
U32 = mybir.dt.uint32
AX = mybir.AxisListType

P = 128
EPS = 1e-5
MASKED = 1e30
LARGEST = 3e38

Q_PART = [0, 0, 1, 1, 0, 2]
K_PART = [0, 1, 0, 1, 2, 0]
PT_RING = 5
SP_RING = 10
QK_RING = 3
M_BANKS = 3
LAG = 5


class Job:

    def __init__(self, step, kind, b, i, engine):
        self.step, self.kind, self.b, self.i, self.engine = step, kind, b, i, engine


def plan_jobs(B, first):
    jobs = []
    for b in range(B):
        at = 64 * (b - 1)
        steps = [8, 9, 12, 16, 20, 24, 28, 30, 32, 34] if b else [68 - 14 + i for i in range(10)]
        kinds = [("xT", 0, "act"), ("xT", 1, "act"), ("q", 0, "dve"), ("k", 0, "dve"), ("q", 1, "dve"),
                 ("k", 1, "dve"), ("v", 0, "dve"), ("v", 1, "dve"), ("v", 2, "dve"), ("v", 3, "dve")]
        for step, (kind, i, engine) in zip(steps, kinds):
            jobs.append(Job(at + step, kind, b, i, engine))
        for g in range(4):
            jobs.append(Job(64 * b + 16 * (g + 1) + 9.5, "norm", b, g, "dve"))
        at = 64 * (b + 1)
        for i, step in enumerate([11, 13]):
            jobs.append(Job(at + step, "aT", b, i, "act"))
        for i, step in enumerate([15, 17, 18, 19]):
            jobs.append(Job(at + step, "y", b, i, "dve"))
        for i, step in enumerate([27, 29]):
            jobs.append(Job(at + step, "xn2T", b, i, "act"))
        jobs.append(Job(at + 31, "lg", b, 0, "dve"))
        for i in range(4):
            jobs.append(Job(at + 36 + 4 * i, "sg", b, i, "act"))
            jobs.append(Job(at + 38 + 4 * i, "su", b, i, "dve"))
        for i, step in enumerate([53, 55, 57, 59]):
            jobs.append(Job(at + step, "dn", b, i, "dve"))
    jobs.sort(key=lambda j: j.step)
    done = {"act": 0, "dve": 0}
    for n, j in enumerate(jobs):
        j.n = n
        j.step = int(j.step)
        done[j.engine] += 1
        j.done = done[j.engine]
    return jobs


def build(nc, x, ctxT, mask, adj, WqT, bq, WkT, bk, WvT, bv, WoT, bo, gateT, WgT, WuT, WdT,
          SgT, SuT, SdT, out, PHASES=3):
    T, D = x.shape
    B = mask.shape[0]
    S = T // B
    H = 16
    DH = D // H
    E = gateT.shape[1]
    I = WgT.shape[2]
    IS = SgT.shape[1]
    C = 2 * T // E
    NT = T // P
    QT = S // P
    DC = D // P
    UNITS = B * H * QT
    FIRST = -16
    LAST = UNITS + 64

    x_v = x.rearrange("(n p) d -> p n d", p=P)
    out_v = out.rearrange("(n p) d -> p n d", p=P)

    jobs = plan_jobs(B, FIRST)
    job = {(j.kind, j.b, j.i): j for j in jobs}

    norms = sorted([(64 * (b - 1) + (4 if b else 48), 1, b) for b in range(B)]
                   + [(64 * (b + 1) + 21, 2, b) for b in range(B)])
    norm_n = {(which, b): n for n, (_, which, b) in enumerate(norms)}

    with ExitStack() as ctx:
        def sb(name, shape, dt, stack=ctx, side=None):
            return stack.enter_context(nc.sbuf_tensor(name, shape, dt, side=side))

        def sem(name):
            return ctx.enter_context(nc.semaphore(name))

        qk_d = nc.dram_tensor("qk_parts", [B, 2, 3, D, S], BF16, kind="Internal").ap()
        xn2_d = nc.dram_tensor("xn2_rows", [T, D], F32, kind="Internal").ap()

        ps_s = [ctx.enter_context(nc.psum_tensor(f"ps_s{i}", [P, 512], F32)) for i in range(2)]
        ps_t = [ctx.enter_context(nc.psum_tensor(f"ps_t{i}", [P, 512], F32)) for i in range(2)]
        ps_u = ctx.enter_context(nc.psum_tensor("ps_u", [P, 512], F32))
        ps_m = [ctx.enter_context(nc.psum_tensor(f"ps_m{i}", [P, 512], F32)) for i in range(M_BANKS)]

        ident = sb("ident", [P, P], F32)
        logits = sb("logits", [P, NT, E], F32)
        x1 = sb("x1", [P, NT, D], F32)
        att = ExitStack()
        late = ExitStack()
        ctx.enter_context(late)
        ctx.enter_context(att)
        wo = sb("w_o", [P, DC, D], F32, late, "right")
        gate = sb("gate", [P, DC, E], F32, late, "right")
        sg_w, su_w = [sb(f"w_{n}", [P, DC, IS], F32, late, "right") for n in ("sg", "su")]
        sd_w = sb("w_sd", [P, IS // P, D], F32, late, "right")
        bo_b = sb("bo_b", [P, D], F32, late, "right")
        half = sb("half", [P, QT], F32, late, "right")
        xn = sb("xn", [P, QT, D], F32, late, "right")
        xn2T = sb("xn2T", [P, DC, S], F32, late, "right")
        stats = sb("stats", [P, QT, 6], F32, late, "right")
        mv = sb("mv", [P, QT, 2], F32, late, "right")
        rs = sb("rs", [P, 3, QT], F32, late, "right")
        us = sb("us", [P, S], F32, late, "right")
        rc = sb("rc", [P, QT, 4], F32, late, "right")
        o_sb = sb("o_sb", [P, QT, D], F32, late, "right")
        attnT = sb("attnT", [P, DC, S], F32, late, "right")
        gel = sb("gel", [P, S], F32, late, "right")
        hs = sb("hs", [P, IS // P, S], F32, late, "right")
        ctx_sb = sb("ctx_sb", [P, DC, S], F32, att)
        mk = [sb(f"mk{i}", [P, S], F32, att) for i in range(2)]
        am = [sb(f"am{i}", [P, QT, S], F32, att) for i in range(2)]
        wq, wk, wv = [sb(f"w_{n}", [P, DC, D], F32, att) for n in "qkv"]
        bqk = sb("bqk", [P, 2, DC], F32, att)
        bv_b = sb("bv_b", [P, D], F32, att)
        xlnT = sb("xlnT", [P, DC, S], F32, att)
        q32 = [sb(f"q32_{i}", [P, S], F32, att) for i in range(2)]
        parts = [sb(f"parts{i}", [P, 3, S], BF16, att) for i in range(2)]
        qs = [sb(f"qs{i}", [96, 4, S], BF16, att) for i in range(QK_RING)]
        ks = [sb(f"ks{i}", [96, 4, S], BF16, att) for i in range(QK_RING)]
        va = [sb(f"va{i}", [P, QT, H, 32], F32, att) for i in range(2)]
        sp_ = [sb(f"sp{i}", [P, S], F32, att) for i in range(SP_RING)]
        mn = sb("mn", [P, SP_RING], F32, att)
        pt = [sb(f"pt{i}", [P, QT, S], F32, att) for i in range(PT_RING)]

        att.close()

        NSEG = NT // 2
        IC = I // P
        PIECES = 6
        PIECE = DC * I // 2
        BY_POOL = (2, 5)
        probs = sb("probs", [P, 2, NSEG, E], F32)
        soft = sb("soft", [P, NT, E], F32)
        soft1 = sb("soft1", [P, 3, NT], F32)
        ptok = sb("ptok", [P, 2 * P], F32)
        zeros = sb("zeros", [P, 2 * P], F32)
        above = sb("above", [P, 2 * P], F32)
        tied = sb("tied", [P, 2 * P], F32)
        prefix = sb("prefix", [P, 2 * P], F32)
        chosen = sb("chosen", [P, 2 * P], F32)
        same_e = sb("same_e", [P, P], F32)
        earlier = sb("earlier", [P, P], F32)
        bit = sb("bit", [P, 1], I32)
        theta = sb("theta", [P, 1], F32)
        cand = sb("cand", [P, 1], F32)
        cnt = sb("cnt", [P, 4], F32)
        slot_row = sb("slot_row", [P, C], BF16)
        slot_int = sb("slot_int", [P, C], I32)
        tok_int = sb("tok_int", [P, 2, NSEG, E], I32)
        rank = sb("rank", [P, NT, E], F32)
        route = sb("route", [P, NT, E, 5], BF16)
        rank_e = [sb(f"rank_e{i}", [P, NT, 1], F32) for i in range(2)]
        route_e = [sb(f"route_e{i}", [P, NT, 5], BF16) for i in range(2)]
        wres = sb("wres", [P, NT * E], F32)
        hot = [sb(f"hot{i}", [P, NT, C], BF16) for i in range(2)]
        rt = sb("rt", [P, 2, 5], F32)
        idx = [sb(f"idx{i}", [P, 2], U32) for i in range(2)]
        wt = [sb(f"wt{i}", [P, 2, 2], F32) for i in range(2)]
        raw = [sb(f"raw{j}", [P, PIECE], F32) for j in range(PIECES)]
        w_hi = [[sb(f"w_hi{i}_{j}", [P, PIECE], F32R) for j in range(PIECES)] for i in range(2)]
        w_lo_a = [[sb(f"w_lo{i}_{j}", [P, PIECE], F32R) for j in range(PIECES - 2)] for i in range(2)]
        late.close()
        w_lo_b = [[sb(f"w_lo{i}_{j}", [P, PIECE], F32R, side="right") for j in range(PIECES - 2, PIECES)] for i in range(2)]
        w_lo = [a + b for a, b in zip(w_lo_a, w_lo_b)]
        xg = [sb(f"xg{i}", [P, 2, D], F32, side="right") for i in range(2)]
        x_hi = [sb(f"x_hi{i}", [P, DC, C], F32R, side="right") for i in range(2)]
        x_lo = [sb(f"x_lo{i}", [P, DC, C], F32R, side="right") for i in range(2)]
        gl = [sb(f"gl{i}", [P, C], F32, side="right") for i in range(2)]
        hid = [sb(f"hid{i}", [P, C], F32, side="right") for i in range(2)]
        h_hi = sb("h_hi", [P, IC, C], F32R, side="right")
        h_lo = sb("h_lo", [P, IC, C], F32R, side="right")
        eo = [sb(f"eo{i}", [P, 2, D], F32, side="right") for i in range(2)]

        s_top = sem("topk_chain")
        s_softin = sem("logits_shifted")
        s_softex = sem("logits_exp")
        s_probs = sem("probs_ready")
        s_ptokT = sem("probs_turned")
        s_cnt = sem("local_counts")
        s_tot = sem("total_counts")
        s_const = sem("topk_constants")
        s_pos = sem("slots_ready")
        s_posT = sem("slots_turned")
        s_route = sem("route_table")
        s_col = sem("expert_columns")
        s_hot = sem("one_hot_ready")
        s_ri = sem("routed")
        s_rt = sem("routes_chain")
        s_idx = sem("indices_ready")
        s_gath = [sem(f"gathered{i}") for i in range(2)]
        s_xgt = sem("gathered_turned")
        s_xgc = sem("gathered_copied")
        s_raw = [sem(f"piece_in{j}") for j in range(PIECES)]
        s_whi = sem("piece_high_parts")
        s_wlo = {False: sem("piece_low_by_dve"), True: sem("piece_low_by_pool")}
        s_hid = sem("hidden_float32")
        s_hhi = sem("hidden_high_part")
        s_xlo = sem("gathered_low_part")
        s_gu = sem("gate_up_ready")
        s_gl = sem("gelu_ready")
        s_h = sem("hidden_ready")
        s_dn = sem("down_ready")
        s_eo = sem("expert_out_ready")
        s_scat = sem("scattered")

        ps_i, ps_c, ps_d, ps_x = ps_s[0], ps_s[1], ps_m[0], ps_m[1]
        ps_g = [ps_t[0], ps_t[1], ps_u, ps_m[2]]

        def low_parts(eng, e, j):
            pool_n = sum(i <= j for i in BY_POOL)
            if j + 1 - pool_n:
                eng.wait_ge(s_wlo[False], (PIECES - len(BY_POOL)) * e + j + 1 - pool_n)
            if pool_n:
                eng.wait_ge(s_wlo[True], len(BY_POOL) * e + pool_n)

        def low_part(eng, e, k, j):
            eng.wait_ge(s_whi, PIECES * e + j + 1)
            eng.tensor_tensor(w_lo[k][j][:, :], raw[j][:, :], w_hi[k][j][:, :].bitcast(F32), ALU.subtract).then_inc(s_wlo[j in BY_POOL], 1)

        def ps_g_of(k, i):
            return ps_g[(IC * k + i) % len(ps_g)]

        def experts(eng, body):
            for k in range(2):
                body(k, k, 0, False)
            with eng.Fori(1, E // 2 - 1) as p:
                for k in range(2):
                    body(2 * p + k, k, p, False)
            for k in range(2):
                body(E - 2 + k, k, E // 2 - 1, True)

        s_x = [sem(f"x_in{b}") for b in range(B)]
        s_cin = sem("ctx_in")
        s_mask = [sem(f"mask_in{i}") for i in range(2)]
        s_adj = sem("adj_in")
        s_w = sem("attn_weights_in")
        s_wv = sem("value_weights_in")
        s_ws = sem("shared_weights_in")
        s_ident = sem("ident_ready")
        s_setup = sem("setup_done")
        s_pool = sem("pool_chain")
        s_dve = sem("dve_chain")
        s_stat = sem("stats_ready")
        s_rstd = sem("rstd_ready")
        s_xn = sem("normed_ready")
        s_am = sem("am_ready")
        s_xb = sem("x_plus_bias")
        s_parts0 = sem("first_parts_ready")
        s_parts = sem("parts_ready")
        s_stored = [sem(f"parts_stored{i}") for i in range(2)]
        s_qkin = [sem(f"qk_in{i}") for i in range(QK_RING)]
        s_score = sem("score_ready")
        s_added = sem("masked_scores_ready")
        s_exp = sem("exp_ready")
        s_tr = sem("transposes_ready")
        s_eva = sem("pt_by_act")
        s_evd = sem("pt_by_dve")
        s_pv = sem("pv_ready")
        s_us = sem("us_ready")
        s_m = sem("job_filled")
        s_done = {"act": sem("job_emptied_by_act"), "dve": sem("job_emptied_by_dve")}
        s_xst = sem("xn2_stored")
        s_out = sem("out_stored")

        def by_act(s):
            return s % 8 in (0, 2, 3, 5, 6)

        act_before = [0]
        for s in range(LAG, UNITS + LAG):
            act_before.append(act_before[-1] + by_act(s))

        def wait_moved(eng, s):
            n = s - LAG + 1
            if act_before[n]:
                eng.wait_ge(s_eva, act_before[n])
            if n - act_before[n]:
                eng.wait_ge(s_evd, n - act_before[n])

        def wait_job(eng, *key):
            j = job[key]
            eng.wait_ge(s_done[j.engine], j.done)

        def parts_made(eng, n):
            eng.wait_ge(*((s_parts0, n + 1) if n < 2 else (s_parts, n - 1)))

        def bank(j):
            return ps_m[j.n % M_BANKS]

        block = ctx.enter_context(nc.Block())

        @block.sync
        def _(sp):
            def load_x(b):
                sp.dma_start(x1[:, QT * b:QT * b + QT, :], x_v[:, QT * b:QT * b + QT, :]).then_inc(s_x[b], 16)

            def load_ctx(b):
                if b:
                    wait_job(sp, "v", b - 1, 3)
                sp.dma_start(ctx_sb[:, :, :], ctxT.rearrange("(c p) t -> p c t", p=P)[:, :, S * b:S * b + S]).then_inc(s_cin, 16)

            def load_adj(b):
                if b >= 2:
                    sp.wait_ge(s_added, 64 * (b - 1))
                sp.dma_start(am[b % 2][:, :, :], adj.rearrange("(n p) k -> p n k", p=P)).then_inc(s_adj, 16)

            def load_mask(b, qt):
                n = QT * b + qt
                if n >= 2:
                    sp.wait_ge(s_am, n - 1)
                sp.dma_start(mk[n % 2][:, :].bitcast(I32), mask[b, P * qt:P * qt + P, :]).then_inc(s_mask[n % 2], 16)

            def store_parts(b, k):
                n = 4 * b + k
                c, which = k // 2, k % 2
                parts_made(sp, n)
                sp.dma_start(qk_d[b, which, :, P * c:P * c + P, :].rearrange("k f t -> f k t"), parts[n % 2][:, :, :]).then_inc(s_stored[n % 2], 16)

            def load_qk(G):
                b, g = G // 4, G % 4
                for i in range(2):
                    sp.wait_ge(s_stored[i], 16 * (2 * b + g // 2 + 1))
                if G >= QK_RING:
                    sp.wait_ge(s_score, 16 * (G - QK_RING + 1))
                for which, (dst, kinds) in enumerate(((qs, Q_PART), (ks, K_PART))):
                    for i, kind in enumerate(kinds):
                        src = qk_d[b, which, kind, 64 * g:64 * g + 64, :].rearrange("(h d) t -> d h t", d=DH)
                        sp.dma_start(dst[G % QK_RING][16 * i:16 * i + 16, :, :], src).then_inc(s_qkin[G % QK_RING], 16)

            load_x(0)
            load_ctx(0)
            for t, src in ((wq, WqT), (wk, WkT)):
                sp.dma_start(t[:, :, :], src.rearrange("(c p) f -> p c f", p=P)).then_inc(s_w, 16)
            for i, src in enumerate((bq, bk)):
                sp.dma_start(bqk[:, i, :], src.rearrange("(c p) -> p c", p=P), allow_slow_non_contiguous=True).then_inc(s_w, 16)
            sp.dma_start(wv[:, :, :], WvT.rearrange("(c p) f -> p c f", p=P)).then_inc(s_wv, 16)
            sp.dma_start(bv_b[:, :], bv.rearrange("(a f) -> a f", a=1).to_broadcast([P, D])).then_inc(s_wv, 16)
            load_adj(0)
            for qt in range(2):
                load_mask(0, qt)
            for s in range(FIRST, LAST):
                if s == -1:
                    for k in range(2):
                        store_parts(0, k)
                    for G in range(2):
                        load_qk(G)
                    for qt in range(2, QT):
                        load_mask(0, qt)
                    for k in range(2, 4):
                        store_parts(0, k)
                    load_qk(2)
                    sp.dma_start(bo_b[:, :], bo.rearrange("(a f) -> a f", a=1).to_broadcast([P, D])).then_inc(s_ws, 16)
                    sp.dma_start(wo[:, :, :], WoT.rearrange("(c p) f -> p c f", p=P)).then_inc(s_ws, 16)
                    for b in range(1, B):
                        load_x(b)
                    for t, src in ((gate, gateT), (sg_w, SgT), (su_w, SuT), (sd_w, SdT)):
                        sp.dma_start(t[:, :, :], src.rearrange("(c p) f -> p c f", p=P)).then_inc(s_ws, 16)
                b, r = s // 64 + 1, s % 64
                if 0 < b < B:
                    if r == 0:
                        load_ctx(b)
                    if r == 2:
                        load_adj(b)
                    if r in (2, 3, 36, 44):
                        load_mask(b, (2, 3, 36, 44).index(r))
                    if r in (16, 20, 24, 28):
                        store_parts(b, (r - 16) // 4)
                if (s + 28) % 16 == 0 and QK_RING <= (s + 28) // 16 < 4 * B:
                    load_qk((s + 28) // 16)
                b = s // 64 - 1
                if b >= 0 and s % 64 == 24:
                    sp.wait_ge(s_xn, norm_n[2, b] + 1)
                    sp.dma_start(xn2_d.rearrange("(n p) d -> p n d", p=P)[:, QT * b:QT * b + QT, :], xn[:, :, :]).then_inc(s_xst, 16)
                if b >= 0 and s % 64 == 62:
                    wait_job(sp, "dn", b, 3)
                    sp.dma_start(out_v[:, QT * b:QT * b + QT, :], x1[:, QT * b:QT * b + QT, :]).then_inc(s_out, 16)
            sp.wait_ge(s_xst, 16 * B)

            def load(e, j):
                if j < 4:
                    src = (WgT, WuT)[j % 2][e].rearrange("(c p) i -> p c i", p=P)[:, :, I // 2 * (j // 2):I // 2 * (j // 2) + I // 2]
                    dst = raw[j][:, :].rearrange("p (c i) -> p c i", c=DC)
                else:
                    src = WdT[e].rearrange("(c p) d -> p c d", p=P)[:, IC // 2 * (j - 4):IC // 2 * (j - 4) + IC // 2, :]
                    dst = raw[j][:, :].rearrange("p (c d) -> p c d", d=D)
                sp.dma_start(dst, src).then_inc(s_raw[j], 16)

            def body(e, k, p, last):
                if not last:
                    for j in range(PIECES):
                        low_parts(sp, e + 1, j)
                        load(e + 2, j)

            sp.wait_ge(s_us, 4 * B)
            for j in range(PIECES):
                load(0, j)
            for j in range(PIECES):
                low_parts(sp, 0, j)
                load(1, j)
            for e in range(E):
                body(e, e % 2, e // 2, e >= E - 2)

        @block.gpsimd
        def _(pool):
            chain = [0]

            def link(ins):
                chain[0] += 1
                ins.then_inc(s_pool, 1)
                pool.wait_ge(s_pool, chain[0])

            link(pool.memset(ident[:, :], 0.0))
            pool.affine_select(out=ident[:, :], in_=ident[:, :], compare_op=ALU.not_equal, fill=1.0,
                               base=0, pattern=[[-1, P]], channel_multiplier=1).then_inc(s_ident, 1)
            pool.memset(half[:, :], -0.5).then_inc(s_setup, 1)
            for i in range(2):
                link(pool.memset(va[i][:, :, :, DH:32], 0.0))
                pool.memset(va[i][:, :, :, DH:DH + 1], 1.0).then_inc(s_setup, 1)
            pool.wait_ge(s_setup, 3)

            def rstd(n):
                pool.wait_ge(s_stat, n + 1)
                link(pool.tensor_scalar(rs[:, 1, :], mv[:, :, 1], EPS, None, ALU.add))
                link(pool.tensor_tensor(rs[:, 0, :], rs[:, 1, :], half[:, :], ALU.pow))
                link(pool.tensor_tensor(rs[:, 2, :], rs[:, 0, :], rs[:, 0, :], ALU.mult))
                link(pool.tensor_tensor(rs[:, 2, :], rs[:, 2, :], rs[:, 1, :], ALU.mult))
                link(pool.tensor_scalar(rs[:, 2, :], rs[:, 2, :], -0.5, 1.5, ALU.mult, ALU.add))
                pool.tensor_tensor(rs[:, 0, :], rs[:, 0, :], rs[:, 2, :], ALU.mult).then_inc(s_rstd, 1)

            def split(b, k):
                n = 4 * b + k
                wait_job(pool, "qk"[k % 2], b, k // 2)
                if n >= 2:
                    pool.wait_ge(s_stored[n % 2], 16 * (n // 2))
                q, p = q32[n % 2], parts[n % 2]
                link(pool.tensor_copy(p[:, 0, :], q[:, :]))
                link(pool.tensor_tensor(q[:, :], q[:, :], p[:, 0, :], ALU.subtract))
                link(pool.tensor_copy(p[:, 1, :], q[:, :]))
                pool.tensor_tensor(p[:, 2, :], q[:, :], p[:, 1, :], ALU.subtract).then_inc(s_parts, 1)

            def build_am(b, qt):
                n = QT * b + qt
                pool.wait_ge(s_mask[n % 2], 16 * (n // 2 + 1))
                if qt == 0:
                    pool.wait_ge(s_adj, 16 * (b + 1))
                m, a = mk[n % 2], am[b % 2][:, qt, :]
                link(pool.tensor_scalar(m[:, :], m[:, :].bitcast(I32), 0.0, MASKED, ALU.is_equal, ALU.mult))
                pool.tensor_tensor(a, m[:, :], a, ALU.subtract).then_inc(s_am, 1)

            def add_bias(b):
                if b == 0:
                    pool.wait_ge(s_ws, 16 * 6)
                pool.wait_ge(s_xn, norm_n[1, b] + 1)
                for t in range(QT * b, QT * b + QT):
                    i = pool.tensor_tensor(x1[:, t, :], x1[:, t, :], bo_b[:, :], ALU.add)
                i.then_inc(s_xb, 1)

            for s in range(FIRST, LAST):
                for n, (at, which, b) in enumerate(norms):
                    if at == s:
                        rstd(n)
                b, r = s // 64 + 1, s % 64
                if s == -1:
                    for qt in range(2):
                        build_am(0, qt)
                    for k in range(2, 4):
                        split(0, k)
                    for qt in range(2, QT):
                        build_am(0, qt)
                    add_bias(0)
                if 0 < b < B:
                    if r in (14, 18, 22, 26):
                        split(b, (r - 14) // 4)
                    if r in (30, 34, 40, 48):
                        build_am(b, (30, 34, 40, 48).index(r))
                    if r == 36:
                        add_bias(b)

            pool.wait_ge(s_us, 4 * B)
            link(pool.iota(tok_int[:, :, :, :], [[P, 2], [2 * P, NSEG], [0, E]], base=0, channel_multiplier=0))
            link(pool.tensor_copy(route[:, :, :, 0], tok_int[:, :, :, :].rearrange("p h s e -> p (h s) e")))
            link(pool.iota(tok_int[:, :, :, :], [[0, 2], [0, NSEG], [0, E]], base=0, channel_multiplier=1))
            link(pool.tensor_copy(route[:, :, :, 1], tok_int[:, :, :, :].rearrange("p h s e -> p (h s) e")))
            link(pool.iota(slot_int[:, :], [[1, C]], base=1, channel_multiplier=0))
            link(pool.tensor_copy(slot_row[:, :], slot_int[:, :]))
            link(pool.memset(same_e[:, :], 0.0))
            for m in range(1 - NSEG, NSEG):
                link(pool.affine_select(out=same_e[:, :], in_=same_e[:, :], compare_op=ALU.not_equal, fill=1.0,
                                        base=-E * m, pattern=[[-1, P]], channel_multiplier=1))
            link(pool.affine_select(out=earlier[:, :], in_=same_e[:, :], compare_op=ALU.is_gt, fill=0.0,
                                    base=0, pattern=[[1, P]], channel_multiplier=-1))
            pool.memset(zeros[:, :], 0.0).then_inc(s_const, 1)

            def gather(e, k, p):
                pool.wait_ge(s_idx, e + 1)
                pool.wait_ge(s_xst, 16 * B)
                for ch in range(2):
                    pool.indirect_dma_start(out=xg[k][:, ch, :], out_offset=None, in_=xn2_d,
                                            in_offset=bass.IndirectOffsetOnAxis(ap=idx[k][:, ch:ch + 1], axis=0)).then_inc(s_gath[k], 16)

            def scatter(e, k):
                pool.wait_ge(s_eo, e + 1)
                if not isinstance(e, int) or e:
                    pool.wait_ge(s_scat, 32 * e)
                pool.wait_ge(s_out, 16 * B)
                for ch in range(2):
                    pool.indirect_dma_start(out=out, out_offset=bass.IndirectOffsetOnAxis(ap=idx[k][:, ch:ch + 1], axis=0),
                                            in_=eo[k][:, ch, :], in_offset=None,
                                            compute_op=ALU.add).then_inc(s_scat, 16)

            def body(e, k, p, last):
                if not last:
                    gather(e + 1, 1 - k, p + k)
                    for j in BY_POOL:
                        low_part(pool, e + 1, 1 - k, j)
                scatter(e, k)

            for j in BY_POOL:
                low_part(pool, 0, 0, j)
            gather(0, 0, 0)
            for e in range(E):
                body(e, e % 2, e // 2, e == E - 1)
            pool.wait_ge(s_scat, 32 * E)

        @block.scalar
        def _(act):
            def exp(u):
                act.wait_ge(s_added, u + 1)
                act.activation(sp_[u % SP_RING][:, :], sp_[u % SP_RING][:, :], ACT.Exp, bias=mn[:, u % SP_RING:u % SP_RING + 1], scale=-1.0).then_inc(s_exp, 1)

            def move_pt(s):
                h, kt = (s - LAG) // 4, (s - LAG) % 4
                act.wait_ge(s_tr, s - LAG + 1)
                if h >= PT_RING:
                    act.wait_ge(s_pv, 4 * ((h - PT_RING) // 4 + 1))
                act.activation(pt[h % PT_RING][:, kt, :], ps_t[s % 2][:, :], ACT.Copy).then_inc(s_eva, 1)

            def empty(j):
                act.wait_ge(s_m, j.n + 1)
                m = bank(j)
                if j.kind == "xT":
                    if j.b:
                        wait_job(act, "k", j.b - 1, 1)
                    i = act.activation(xlnT[:, j.i, :], m[:, :], ACT.Copy)
                if j.kind == "aT":
                    if j.b:
                        wait_job(act, "y", j.b - 1, 3)
                    i = act.activation(attnT[:, j.i, :], m[:, :], ACT.Copy)
                if j.kind == "xn2T":
                    if j.b:
                        wait_job(act, "su", j.b - 1, 3)
                    i = act.activation(xn2T[:, j.i, :], m[:, :], ACT.Copy)
                if j.kind == "sg":
                    if j.b or j.i:
                        wait_job(act, "su", j.b if j.i else j.b - 1, (j.i + 3) % 4)
                    i = act.activation(gel[:, :], m[:, :], ACT.Gelu)
                i.then_inc(s_done["act"], 1)

            for s in range(FIRST, LAST):
                if 0 <= s - 1 < UNITS:
                    exp(s - 1)
                if LAG <= s - 1 < UNITS + LAG and by_act(s - 1):
                    move_pt(s - 1)
                G = s // 16 - 1
                if s % 16 == 8 and 0 <= G < 4 * B:
                    act.wait_ge(s_pv, 4 * (G + 1))
                    if G:
                        act.wait_ge(s_m, job["norm", (G - 1) // 4, (G - 1) % 4].n + 1)
                    act.activation(us[:, :], ps_u[:, :], ACT.Copy).then_inc(s_us, 1)
                for j in jobs:
                    if j.step == s - 1 and j.engine == "act":
                        empty(j)

            act.wait_ge(s_softin, 1)
            act.activation(soft[:, :, :], soft[:, :, :], ACT.Exp).then_inc(s_softex, 1)

            def copy_gathered(e, k):
                act.wait_ge(s_xgt, e + 1)
                if not isinstance(e, int) or e >= 2:
                    act.wait_ge(s_gu, IC * (e - 1))
                act.activation(x_hi[k][:, :, :], ps_x[:, :].rearrange("p (c t) -> p c t", c=DC), ACT.Copy).then_inc(s_xgc, 1)

            def high_part(e, k, j):
                act.wait_ge(s_raw[j], 16 * (e + 1))
                if not isinstance(e, int) or e >= 2:
                    if j < 4:
                        act.wait_ge(s_gu, IC * (e - 2) + (4 if j < 2 else 8))
                    else:
                        act.wait_ge(s_dn, e - 1)
                act.activation(w_hi[k][j][:, :], raw[j][:, :], ACT.Copy).then_inc(s_whi, 1)

            def hidden_high(e, i):
                act.wait_ge(s_hid, IC * e + i + 1)
                if i == 0 and (not isinstance(e, int) or e):
                    act.wait_ge(s_dn, e)
                act.activation(h_hi[:, i, :], hid[i % 2][:, :], ACT.Copy).then_inc(s_hhi, 1)

            def body(e, k, p, last):
                for i in range(IC):
                    act.wait_ge(s_gu, IC * e + i + 1)
                    if not isinstance(p, int) or p or k or i >= 2:
                        act.wait_ge(s_hid, IC * e + i - 1)
                    act.activation(gl[i % 2][:, :], ps_g_of(k, i)[:, 0:C], ACT.Gelu).then_inc(s_gl, 1)
                    if i:
                        hidden_high(e, i - 1)
                    if i < PIECES and not (last and k == 1):
                        high_part(e + 1, 1 - k, i)
                hidden_high(e, IC - 1)
                if not (last and k == 1):
                    copy_gathered(e + 1, 1 - k)

            for j in range(PIECES):
                high_part(0, 0, j)
            copy_gathered(0, 0)
            experts(act, body)

        @block.vector
        def _(dve):
            chain = [0]

            def link(ins):
                chain[0] += 1
                ins.then_inc(s_dve, 1)
                dve.wait_ge(s_dve, chain[0])

            def add_mask(u):
                b, qt = u // 64, u % 4
                dve.wait_ge(s_score, u + 1)
                if u % 64 < QT:
                    dve.wait_ge(s_am, QT * b + qt + 1)
                if u >= SP_RING:
                    dve.wait_ge(s_tr, 4 * ((u - SP_RING) // 4 + 1))
                dve.tensor_tensor_reduce(sp_[u % SP_RING][:, :], ps_s[u % 2][:, :], am[b % 2][:, qt, :], 1.0, LARGEST,
                                         ALU.add, ALU.min, mn[:, u % SP_RING:u % SP_RING + 1]).then_inc(s_added, 1)

            def move_pt(s):
                h, kt = (s - LAG) // 4, (s - LAG) % 4
                dve.wait_ge(s_tr, s - LAG + 1)
                if h >= PT_RING:
                    dve.wait_ge(s_pv, 4 * ((h - PT_RING) // 4 + 1))
                dve.tensor_copy(pt[h % PT_RING][:, kt, :], ps_t[s % 2][:, :]).then_inc(s_evd, 1)

            def statistics(n, b):
                if n:
                    dve.wait_ge(s_xn, n)
                for t in range(QT):
                    i = dve.bn_stats(stats[:, t, :], x1[:, QT * b + t, :])
                link(i)
                for t in range(QT):
                    i = dve.bn_aggr(mv[:, t, :], stats[:, t, :])
                i.then_inc(s_stat, 1)

            def apply(n, which, b):
                dve.wait_ge(s_rstd, n + 1)
                if n:
                    _, w, pb = norms[n - 1]
                    dve.wait_ge(s_m, job["xT" if w == 1 else "xn2T", pb, 1].n + 1)
                    stored = sum(1 for _, w, _ in norms[:n] if w == 2)
                    if stored:
                        dve.wait_ge(s_xst, 16 * stored)
                for t in range(QT):
                    i = dve.tensor_scalar(xn[:, t, :], x1[:, QT * b + t, :], mv[:, t, 0:1], rs[:, 0, t:t + 1],
                                          ALU.subtract, ALU.mult)
                i.then_inc(s_xn, 1)

            def empty(j):
                dve.wait_ge(s_m, j.n + 1)
                m, b, i = bank(j), j.b, j.i
                if j.kind in "qk":
                    k = 2 * i + (j.kind == "k")
                    n = 4 * b + k
                    if n >= 2:
                        parts_made(dve, n - 2)
                    which = int(j.kind == "k")
                    scale = -1.0 / DH ** 0.5 if j.kind == "q" else 1.0
                    last = dve.tensor_scalar(q32[n % 2][:, :], m[:, :], bqk[:, which, i:i + 1], scale, ALU.add, ALU.mult)
                if j.kind == "v":
                    if b >= 2:
                        dve.wait_ge(s_pv, 16 * (b - 1))
                    last = dve.tensor_tensor(va[b % 2][:, i, :, 0:DH], m[:, 0:D].rearrange("p (h d) -> p h d", h=H),
                                             bv_b[:, :].rearrange("p (h d) -> p h d", h=H), ALU.add)
                if j.kind == "norm":
                    mm = m[:, :].rearrange("p (q j r) -> p q j r", q=QT, r=32)
                    if b and i == 0:
                        dve.wait_ge(s_m, job["aT", b - 1, 1].n + 1)
                    link(dve.reciprocal(rc[:, :, :], mm[:, :, :, DH]))
                    last = dve.tensor_tensor(o_sb[:, :, 64 * i:64 * i + 64].rearrange("p q (j d) -> p q j d", d=DH),
                                             mm[:, :, :, 0:DH], rc[:, :, :].unsqueeze(3).to_broadcast([P, QT, 4, DH]), ALU.mult)
                if j.kind == "y":
                    if i == 0:
                        dve.wait_ge(s_xb, b + 1)
                    last = dve.tensor_tensor(x1[:, QT * b + i, :], m[:, 0:D], x1[:, QT * b + i, :], ALU.add)
                if j.kind == "lg":
                    last = dve.tensor_copy(logits[:, QT * b:QT * b + QT, :], m[:, 0:QT * E].rearrange("p (q e) -> p q e", e=E))
                if j.kind == "su":
                    wait_job(dve, "sg", b, i)
                    if b and i == 0:
                        dve.wait_ge(s_m, job["dn", b - 1, 3].n + 1)
                    last = dve.tensor_tensor(hs[:, i, :], m[:, :], gel[:, :], ALU.mult)
                if j.kind == "dn":
                    last = dve.tensor_tensor(x1[:, QT * b + i, :], m[:, 0:D], x1[:, QT * b + i, :], ALU.add)
                last.then_inc(s_done["dve"], 1)
                if j.kind in "qk" and n < 2:
                    wait_job(dve, j.kind, b, i)
                    q, p = q32[n], parts[n]
                    link(dve.tensor_copy(p[:, 0, :], q[:, :]))
                    link(dve.tensor_tensor(q[:, :], q[:, :], p[:, 0, :], ALU.subtract))
                    link(dve.tensor_copy(p[:, 1, :], q[:, :]))
                    dve.tensor_tensor(p[:, 2, :], q[:, :], p[:, 1, :], ALU.subtract).then_inc(s_parts0, 1)

            for b in range(B):
                pass
            for s in range(FIRST, LAST):
                if s == -14:
                    dve.wait_ge(s_w, 16 * 4)
                    dve.wait_ge(s_wv, 16 * 2)
                    dve.wait_ge(s_setup, 3)
                if 0 <= s < UNITS:
                    add_mask(s)
                if LAG <= s - 1 < UNITS + LAG and not by_act(s - 1):
                    move_pt(s - 1)
                for n, (at, which, b) in enumerate(norms):
                    if at == s:
                        if which == 1:
                            dve.wait_ge(s_x[b], 16)
                        else:
                            wait_job(dve, "y", b, 3)
                        statistics(n, b)
                    if at + 2 == s:
                        apply(n, which, b)
                for j in jobs:
                    if j.step == s - 1 and j.engine == "dve":
                        empty(j)

            top = [0]

            def then(ins):
                top[0] += 1
                ins.then_inc(s_top, 1)
                dve.wait_ge(s_top, top[0])

            dve.wait_ge(s_us, 4 * B)
            then(dve.tensor_reduce(soft1[:, 0, :], logits[:, :, :], AX.X, ALU.max))
            dve.tensor_tensor(soft[:, :, :], logits[:, :, :], soft1[:, 0, :].unsqueeze(2).to_broadcast([P, NT, E]), ALU.subtract).then_inc(s_softin, 1)
            dve.wait_ge(s_softex, 1)
            then(dve.tensor_reduce(soft1[:, 1, :], soft[:, :, :], AX.X, ALU.add))
            then(dve.reciprocal(soft1[:, 2, :], soft1[:, 1, :]))
            dve.tensor_tensor(probs[:, :, :, :], soft[:, :, :].rearrange("p (s h) e -> p h s e", h=2),
                              soft1[:, 2, :].rearrange("p (s h) -> p h s", h=2).unsqueeze(3).to_broadcast([P, 2, NSEG, E]), ALU.mult).then_inc(s_probs, 1)
            dve.wait_ge(s_probs, 1)
            flat = probs[:, :, :, :].rearrange("p h s e -> p (h s e)")
            flat_route = route[:, :, :, :].rearrange("p n e k -> p (n e) k")
            dve.wait_ge(s_const, 1)
            then(dve.tensor_copy(flat_route[:, :, 2], flat))
            then(dve.tensor_tensor(wres[:, :], flat, flat_route[:, :, 2], ALU.subtract))
            then(dve.tensor_copy(flat_route[:, :, 3], wres[:, :]))
            dve.tensor_tensor(flat_route[:, :, 4], wres[:, :], flat_route[:, :, 3], ALU.subtract).then_inc(s_route, 1)

            then(dve.memset(bit[:, :], 1 << 29))
            then(dve.memset(theta[:, :], 0.0))
            dve.wait_ge(s_ptokT, 1)
            then(dve.tensor_copy(ptok[:, :], ps_i[:, 0:2 * P]))
            ROUNDS = 30
            with dve.Fori(0, ROUNDS) as n:
                STEPS = 4
                at = top[0] + STEPS * n
                dve.tensor_tensor(cand[:, :].bitcast(I32), theta[:, :].bitcast(I32), bit[:, :], ALU.bitwise_or).then_inc(s_top, 1)
                dve.wait_ge(s_top, at + 1)
                dve.tensor_scalar(prefix[:, :], ptok[:, :], cand[:, 0:1], 0.0, ALU.is_ge, ALU.add, accum_out=cnt[:, 0:1]).then_inc(s_cnt, 1)
                dve.tensor_scalar(bit[:, :], bit[:, :], 1, None, ALU.logical_shift_right).then_inc(s_top, 1)
                dve.wait_ge(s_tot, n + 1)
                dve.tensor_scalar(cnt[:, 1:2], ps_c[:, 0:1], float(C), cand[:, 0:1], ALU.is_ge, ALU.mult).then_inc(s_top, 1)
                dve.wait_ge(s_top, at + 3)
                dve.tensor_tensor(theta[:, :], theta[:, :], cnt[:, 1:2], ALU.max).then_inc(s_top, 1)
                dve.wait_ge(s_top, at + 4)
            top[0] += STEPS * ROUNDS
            then(dve.tensor_scalar(above[:, :], ptok[:, :], theta[:, 0:1], 0.0, ALU.is_gt, ALU.add, accum_out=cnt[:, 0:1]))
            then(dve.tensor_scalar(tied[:, :], ptok[:, :], theta[:, 0:1], 0.0, ALU.is_equal, ALU.add, accum_out=cnt[:, 1:2]))
            dve.tensor_tensor_scan(prefix[:, :], tied[:, :], zeros[:, :], 0.0, ALU.add, ALU.add).then_inc(s_cnt, 1)
            dve.wait_ge(s_tot, ROUNDS + 1)
            then(dve.tensor_copy(cnt[:, 2:4], ps_c[:, 0:2]))
            then(dve.tensor_tensor(cnt[:, 2:3], cnt[:, 2:3], cnt[:, 3:4], ALU.add))
            then(dve.tensor_scalar(cnt[:, 2:3], cnt[:, 2:3], -1.0, float(C), ALU.mult, ALU.add))
            dve.wait_ge(s_cnt, ROUNDS + 1)
            then(dve.scalar_tensor_tensor(tied[:, :], prefix[:, :], cnt[:, 2:3], tied[:, :], ALU.is_le, ALU.mult))
            dve.scalar_tensor_tensor(chosen[:, :], tied[:, :], 1.0, above[:, :], ALU.mult, ALU.add, accum_out=cnt[:, 0:1]).then_inc(s_cnt, 1)
            dve.wait_ge(s_cnt, ROUNDS + 2)
            then(dve.tensor_tensor_scan(prefix[:, :], chosen[:, :], zeros[:, :], 0.0, ALU.add, ALU.add))
            dve.wait_ge(s_tot, ROUNDS + 2)
            dve.scalar_tensor_tensor(prefix[:, :], prefix[:, :], ps_c[:, 0:1], chosen[:, :], ALU.add, ALU.mult).then_inc(s_pos, 1)
            dve.wait_ge(s_posT, 1)
            then(dve.tensor_copy(rank[:, :, :], ps_i[:, 0:2 * P].rearrange("p (n e) -> p n e", e=E)))

            def one_hot(e, k):
                if not isinstance(e, int) or e >= 2:
                    dve.wait_ge(s_ri, e - 1)
                dve.tensor_copy(rank_e[k][:, :, :], rank[:, :, bass.ds(e, 1)]).then_inc(s_col, 1)
                dve.tensor_copy(route_e[k][:, :, :], route[:, :, bass.ds(e, 1), :].rearrange("p n a k -> p n (a k)"))
                dve.wait_ge(s_col, e + 1)
                for n in range(NT):
                    i = dve.tensor_scalar(hot[k][:, n, :], slot_row[:, :], rank_e[k][:, n, :], None, ALU.is_equal)
                i.then_inc(s_hot, 1)

            def take_routes(e, k):
                dve.wait_ge(s_ri, e + 1)
                r = ps_i[:, 0:10].rearrange("p (c k) -> p c k", k=5)
                if not isinstance(e, int) or e >= 2:
                    dve.wait_ge(s_scat, 32 * (e - 1))
                dve.tensor_copy(rt[:, :, :], r).then_inc(s_rt, 1)
                dve.wait_ge(s_rt, 2 * e + 1)
                dve.tensor_tensor(idx[k][:, :], rt[:, :, 0], rt[:, :, 1], ALU.add)
                dve.tensor_tensor(wt[k][:, 0, :], rt[:, :, 2], rt[:, :, 3], ALU.add).then_inc(s_rt, 1)
                dve.wait_ge(s_rt, 2 * e + 2)
                dve.tensor_tensor(wt[k][:, 1, :], wt[k][:, 0, :], rt[:, :, 4], ALU.add).then_inc(s_idx, 1)

            def gathered_low(e, k):
                dve.wait_ge(s_xgc, e + 1)
                dve.tensor_tensor(x_lo[k][:, :, :], ps_x[:, :].rearrange("p (c t) -> p c t", c=DC),
                                  x_hi[k][:, :, :].bitcast(F32), ALU.subtract).then_inc(s_xlo, 1)

            def hidden_low(e, i):
                dve.wait_ge(s_hhi, IC * e + i + 1)
                dve.tensor_tensor(h_lo[:, i, :], hid[i % 2][:, :], h_hi[:, i, :].bitcast(F32), ALU.subtract).then_inc(s_h, 1)

            def body(e, k, p, last):
                for i in range(IC):
                    if i == 2 and not (last and k == 1):
                        take_routes(e + 1, 1 - k)
                    dve.wait_ge(s_gl, IC * e + i + 1)
                    if not isinstance(p, int) or p or k or i >= 2:
                        dve.wait_ge(s_h, IC * e + i - 1)
                    dve.tensor_tensor(hid[i % 2][:, :], ps_g_of(k, i)[:, C:2 * C], gl[i % 2][:, :], ALU.mult).then_inc(s_hid, 1)
                    if i:
                        hidden_low(e, i - 1)
                    if i < PIECES and i not in BY_POOL and not (last and k == 1):
                        low_part(dve, e + 1, 1 - k, i)
                hidden_low(e, IC - 1)
                if not (last and k == 1):
                    gathered_low(e + 1, 1 - k)
                if not last:
                    one_hot(e + 2, k)
                dve.wait_ge(s_dn, e + 1)
                dve.wait_ge(s_idx, e + 1)
                for ch in range(2):
                    i = dve.tensor_scalar(eo[k][:, ch, :], ps_d[:, D * ch:D * ch + D], wt[k][:, 1, ch:ch + 1], None, ALU.mult)
                i.then_inc(s_eo, 1)

            one_hot(0, 0)
            one_hot(1, 1)
            take_routes(0, 0)
            for j in range(PIECES):
                if j not in BY_POOL:
                    low_part(dve, 0, 0, j)
            gathered_low(0, 0)
            experts(dve, body)

        @block.tensor
        def _(pe):
            def score(u):
                G, h, qt = u // 16, (u // 4) % 4, u % 4
                if u % 16 == 0:
                    pe.wait_ge(s_qkin[G % QK_RING], 16 * 12 * (G // QK_RING + 1))
                if u >= 2:
                    pe.wait_ge(s_added, u - 1)
                pe.matmul(ps_s[u % 2][:, :], qs[G % QK_RING][:, h, P * qt:P * qt + P], ks[G % QK_RING][:, h, :],
                          start=True, stop=True).then_inc(s_score, 1)

            def transposes(s):
                h, kt = (s - LAG) // 4, (s - LAG) % 4
                if kt == 0:
                    pe.wait_ge(s_exp, 4 * h + 4)
                if s - 2 >= LAG:
                    wait_moved(pe, s - 2)
                for qt in range(QT):
                    i = pe.transpose(ps_t[s % 2][:, P * qt:P * qt + P], sp_[(4 * h + qt) % SP_RING][:, P * kt:P * kt + P], ident[:, :])
                i.then_inc(s_tr, 1)

            def pv(G, kt):
                if kt == 0 and G:
                    pe.wait_ge(s_us, G)
                wait_moved(pe, 4 * (4 * G + 3) + LAG + kt)
                b, g = G // 4, G % 4
                for j in range(4):
                    i = pe.matmul(ps_u[32 * j:32 * j + 32, :], va[b % 2][:, kt, 4 * g + j, :], pt[(4 * G + j) % PT_RING][:, kt, :],
                                  start=(kt == 0), stop=(kt == 3))
                i.then_inc(s_pv, 1)

            def fill(j):
                m, b, i = bank(j), j.b, j.i
                if j.n >= M_BANKS:
                    e = jobs[j.n - M_BANKS]
                    pe.wait_ge(s_done[e.engine], e.done)
                if j.kind in ("xT", "xn2T"):
                    pe.wait_ge(s_xn, norm_n[1 if j.kind == "xT" else 2, b] + 1)
                    for t in range(QT):
                        last = pe.transpose(m[:, P * t:P * t + P], xn[:, t, P * i:P * i + P], ident[:, :])
                if j.kind in "qk":
                    wait_job(pe, "xT", b, 1)
                    pe.wait_ge(s_cin, 16 * (b + 1))
                    if b == 0 and i == 0:
                        pe.wait_ge(s_w, 16 * 4)
                    w, src = (wq, xlnT) if j.kind == "q" else (wk, ctx_sb)
                    for c in range(DC):
                        last = pe.matmul(m[:, :], w[:, c, P * i:P * i + P], src[:, c, :], start=(c == 0), stop=(c == DC - 1))
                if j.kind == "v":
                    if b == 0 and i == 0:
                        pe.wait_ge(s_wv, 16 * 2)
                    for c in range(DC):
                        last = pe.matmul(m[:, 0:D], ctx_sb[:, c, P * i:P * i + P], wv[:, c, :], start=(c == 0), stop=(c == DC - 1))
                if j.kind == "norm":
                    pe.wait_ge(s_us, 4 * b + i + 1)
                    for t in range(QT):
                        last = pe.transpose(m[:, P * t:P * t + P], us[:, P * t:P * t + P], ident[:, :])
                if j.kind == "aT":
                    wait_job(pe, "norm", b, 3)
                    for t in range(QT):
                        last = pe.transpose(m[:, P * t:P * t + P], o_sb[:, t, P * i:P * i + P], ident[:, :])
                if j.kind == "y":
                    wait_job(pe, "aT", b, 1)
                    if b == 0 and i == 0:
                        pe.wait_ge(s_ws, 16 * 6)
                    for c in range(DC):
                        last = pe.matmul(m[:, 0:D], attnT[:, c, P * i:P * i + P], wo[:, c, :], start=(c == 0), stop=(c == DC - 1))
                if j.kind == "lg":
                    wait_job(pe, "xn2T", b, 1)
                    for t in range(QT):
                        for c in range(DC):
                            last = pe.matmul(m[:, E * t:E * t + E], xn2T[:, c, P * t:P * t + P], gate[:, c, :], start=(c == 0), stop=(c == DC - 1))
                if j.kind in ("sg", "su"):
                    wait_job(pe, "xn2T", b, 1)
                    w = sg_w if j.kind == "sg" else su_w
                    for c in range(DC):
                        last = pe.matmul(m[:, :], w[:, c, P * i:P * i + P], xn2T[:, c, :], start=(c == 0), stop=(c == DC - 1))
                if j.kind == "dn":
                    wait_job(pe, "su", b, 3)
                    for c in range(IS // P):
                        last = pe.matmul(m[:, 0:D], hs[:, c, P * i:P * i + P], sd_w[:, c, :], start=(c == 0), stop=(c == IS // P - 1))
                last.then_inc(s_m, 1)

            pe.wait_ge(s_ident, 1)
            for s in range(FIRST, LAST):
                if s == 0:
                    pe.wait_ge(s_setup, 3)
                if 0 <= s < UNITS:
                    score(s)
                if LAG <= s < UNITS + LAG:
                    transposes(s)
                G = s // 16 - 1
                if 0 <= G < 4 * B and 4 <= s % 16 < 8:
                    pv(G, s % 16 - 4)
                for j in jobs:
                    if j.step == s:
                        fill(j)

            pe.wait_ge(s_probs, 1)
            for hf in range(2):
                i = pe.transpose(ps_i[:, P * hf:P * hf + P], probs[:, hf, :, :].rearrange("p s e -> p (s e)"), ident[:, :])
            i.then_inc(s_ptokT, 1)
            pe.wait_ge(s_const, 1)
            ROUNDS = 30
            with pe.Fori(0, ROUNDS) as n:
                pe.wait_ge(s_cnt, n + 1)
                pe.matmul(ps_c[:, 0:1], same_e[:, :], cnt[:, 0:1], start=True, stop=True).then_inc(s_tot, 1)
            pe.wait_ge(s_cnt, ROUNDS + 1)
            pe.matmul(ps_c[:, 0:1], same_e[:, :], cnt[:, 0:1], start=True, stop=True)
            pe.matmul(ps_c[:, 1:2], earlier[:, :], cnt[:, 1:2], start=True, stop=True).then_inc(s_tot, 1)
            pe.wait_ge(s_cnt, ROUNDS + 2)
            pe.matmul(ps_c[:, 0:1], earlier[:, :], cnt[:, 0:1], start=True, stop=True).then_inc(s_tot, 1)
            pe.wait_ge(s_pos, 1)
            for hf in range(2):
                i = pe.transpose(ps_i[:, P * hf:P * hf + P], prefix[:, P * hf:P * hf + P], ident[:, :])
            i.then_inc(s_posT, 1)
            pe.wait_ge(s_route, 1)

            def routes(e, k):
                pe.wait_ge(s_hot, e + 1)
                if not isinstance(e, int) or e:
                    pe.wait_ge(s_idx, e)
                for ch in range(2):
                    for n in range(NT):
                        i = pe.matmul(ps_i[:, 5 * ch:5 * ch + 5], hot[k][:, n, P * ch:P * ch + P], route_e[k][:, n, :],
                                      start=(n == 0), stop=(n == NT - 1))
                i.then_inc(s_ri, 1)

            def exact(out, a_hi, a_lo, b_hi, b_lo, start, stop):
                pe.matmul(out, a_hi, b_hi, start=start, stop=False)
                pe.matmul(out, a_hi, b_lo, start=False, stop=False)
                return pe.matmul(out, a_lo, b_hi, start=False, stop=stop)

            def turn_gathered(e, k, p):
                pe.wait_ge(s_gath[k], 32 * (p + 1))
                if not isinstance(e, int) or e:
                    pe.wait_ge(s_xlo, e)
                for c in range(DC):
                    for ch in range(2):
                        i = pe.transpose(ps_x[:, C * c + P * ch:C * c + P * ch + P], xg[k][:, ch, P * c:P * c + P], ident[:, :])
                i.then_inc(s_xgt, 1)

            def body(e, k, p, last):
                pe.wait_ge(s_xlo, e + 1)
                for i in range(IC):
                    if i in (0, 4):
                        low_parts(pe, e, 1 + 2 * (i // 4))
                    if i == 2 and not (last and k == 1):
                        routes(e + 1, 1 - k)
                    if not isinstance(p, int) or p or k or i >= len(ps_g):
                        pe.wait_ge(s_hid, IC * e + i - len(ps_g) + 1)
                    for which in range(2):
                        j = 2 * (i // 4) + which
                        for c in range(DC):
                            at = I // 2 * c + P * (i % 4)
                            m = exact(ps_g_of(k, i)[:, C * which:C * which + C], w_hi[k][j][:, at:at + P], w_lo[k][j][:, at:at + P],
                                      x_hi[k][:, c, :], x_lo[k][:, c, :], c == 0, c == DC - 1)
                    m.then_inc(s_gu, 1)
                if not (last and k == 1):
                    turn_gathered(e + 1, 1 - k, p + k)
                low_parts(pe, e, PIECES - 1)
                if not isinstance(p, int) or p or k:
                    pe.wait_ge(s_eo, e)
                for ch in range(2):
                    for i in range(IC):
                        if ch == 0:
                            pe.wait_ge(s_h, IC * e + i + 1)
                        j, at = 4 + i // 4, D * (i % 4)
                        m = exact(ps_d[:, D * ch:D * ch + D], h_hi[:, i, P * ch:P * ch + P], h_lo[:, i, P * ch:P * ch + P],
                                  w_hi[k][j][:, at:at + D], w_lo[k][j][:, at:at + D], i == 0, i == IC - 1)
                m.then_inc(s_dn, 1)

            routes(0, 0)
            turn_gathered(0, 0, 0)
            experts(pe, body)


_OUTS = [((4, 512, 256), "float32")]


def kernel(**inputs):
    import numpy as _np
    import concourse.bacc as _bacc
    from concourse import mybir as _mybir
    from concourse.bass_utils import run_bass_kernel_spmd as _run

    a = {k: _np.asarray(v) for k, v in inputs.items()}
    p = {k[len("L0_xattn_"):]: v for k, v in a.items() if k.startswith("L0_xattn_")}
    f = {k[len("L0_ffn_"):]: v for k, v in a.items() if k.startswith("L0_ffn_")}
    x = a["x"]
    d = x.shape[-1]
    arrays = {
        "x": x.reshape(-1, d), "ctxT": a["ctx_1024"].reshape(-1, d).T, "mask": a["mask_Bx1xSxS2_ik1"][:, 0],
        "adj": p["adj"], "WqT": p["Wq"].T, "bq": p["bq"], "WkT": p["Wk"].T, "bk": p["bk"],
        "WvT": p["Wv"].T, "bv": p["bv"], "WoT": p["Wo"].T, "bo": p["bo"], "gateT": f["gate_w"].T,
        "WgT": f["Wg"].transpose(0, 2, 1), "WuT": f["Wu"].transpose(0, 2, 1), "WdT": f["Wd"].transpose(0, 2, 1),
        "SgT": f["Sg"].T, "SuT": f["Su"].T, "SdT": f["Sd"].T,
    }
    arrays = {k: _np.ascontiguousarray(v) for k, v in arrays.items()}
    nc = _bacc.Bacc("TRN2", target_bir_lowering=False, num_devices=1)
    args = [nc.dram_tensor(f"in_{k}", v.shape, _mybir.dt.from_np(v.dtype), kind="ExternalInput").ap()
            for k, v in arrays.items()]
    out = nc.dram_tensor("out_0", [x.shape[0] * x.shape[1], d], F32, kind="ExternalOutput").ap()
    build(nc, *args, out)
    r = _run(nc, [{f"in_{k}": v for k, v in arrays.items()}], core_ids=[0])
    return r.results[0]["out_0"].reshape(x.shape)
```

```python
from contextlib import ExitStack

import concourse.bass as bass
from concourse import mybir

ALU = mybir.AluOpType
ACT = mybir.ActivationFunctionType
F32 = mybir.dt.float32
F32R = mybir.dt.float32r
BF16 = mybir.dt.bfloat16
I32 = mybir.dt.int32
U32 = mybir.dt.uint32
AX = mybir.AxisListType

P = 128
EPS = 1e-5
MASKED = 1e30
LARGEST = 3e38

Q_PART = [0, 0, 0, 1, 1, 2]
K_PART = [0, 1, 2, 0, 1, 0]
PAIR_RUNS = [(0, 3), (3, 5), (5, 6)]
STORES = (len(Q_PART), 3)

BATCH_STEPS = 64
QK_RING = 3
SP_RING = 13
PT_RING = 22
LAG = 7
PV_AT, PV_EVERY = 5, 4
BY_VECTOR = (1, 3, 6, 8, 12, 14)
WARM = {"start": 24, "scores": 20, "norm": 12, "softmax": 0}

PROJECTIONS = [6, 8, 12, 15, 39, 42, 55, 57, 60, 63]
FIRST_PROJECTIONS = [17, 19, 22, 26]
DIVISION = 4
OUTPUTS = [22, 24, 26, 28, 31, 33, 45, 47, 49]
LAST_OUTPUTS = [21, 22, 23, 24, 25, 26, 31, 32, 34]


class Job:

    def __init__(self, step, kind, b, i, engine, edge):
        self.first = step - (kind in "qk" and not edge)
        self.step, self.kind, self.b, self.i, self.engine = step, kind, b, i, engine
        self.edge = edge


def plan_jobs(B):
    jobs = []
    for b in range(B):
        at = BATCH_STEPS * (b - 1)
        steps = list(PROJECTIONS) if b else [BATCH_STEPS - 12 + i for i in range(10)]
        if b == 1:
            steps[:4] = FIRST_PROJECTIONS
        kinds = [("xT", 0, "act"), ("xT", 1, "act"), ("q", 0, "dve"), ("k", 0, "dve"), ("q", 1, "dve"),
                 ("k", 1, "dve"), ("v", 0, "dve"), ("v", 1, "dve"), ("v", 2, "dve"), ("v", 3, "dve")]
        for step, (kind, i, engine) in zip(steps, kinds):
            jobs.append(Job(at + step, kind, b, i, engine, b == 0))
        last = b == B - 1
        for g in range(4):
            jobs.append(Job(BATCH_STEPS * b + 16 * (g + 2) + DIVISION, "norm", b, g, "dve", last and g == 3))
        at = BATCH_STEPS * (b + 1)
        steps = LAST_OUTPUTS if last else OUTPUTS
        kinds = [("aT", 0, "act"), ("aT", 1, "act"), ("y", 0, "dve"), ("y", 1, "dve"), ("y", 2, "dve"),
                 ("y", 3, "dve"), ("xn2T", 0, "act"), ("xn2T", 1, "act"), ("lg", 0, "dve")]
        for step, (kind, i, engine) in zip(steps, kinds):
            jobs.append(Job(at + step, kind, b, i, engine, last))
    jobs.sort(key=lambda j: j.step)
    norms = [j for j in jobs if j.kind == "norm"]
    for j, before in zip(norms, [None] + norms):
        j.before_norm = before and (before.kind, before.b, before.i)
    done, held, edges = {"act": 0, "dve": 0}, {}, 0
    for n, j in enumerate(jobs):
        j.n = n
        done[j.engine] += 1
        j.done = done[j.engine]
        j.bank = 1 + edges % 2 if j.edge else 0
        edges += j.edge
        j.before = held.get(j.bank)
        held[j.bank] = j
    return jobs


def build(nc, x, ctxT, mask, adj, WqT, bq, WkT, bk, WvT, bv, WoT, bo, gateT, WgT, WuT, WdT,
          SgT, SuT, SdT, out):
    T, D = x.shape
    B = mask.shape[0]
    S = T // B
    H = 16
    DH = D // H
    E = gateT.shape[1]
    I = WgT.shape[2]
    IS = SgT.shape[1]
    C = 2 * T // E
    NT = T // P
    QT = S // P
    DC = D // P
    UNITS = B * H * QT
    FIRST = -16
    LAST = UNITS + 37

    x_v = x.rearrange("(n p) d -> p n d", p=P)
    out_v = out.rearrange("(n p) d -> p n d", p=P)

    jobs = plan_jobs(B)
    job = {(j.kind, j.b, j.i): j for j in jobs}

    norms = [(-16, 1, 0, 2, False), (10, 1, 1, 2, True)]
    norms += [(BATCH_STEPS * (b - 1) - 8, 1, b, 4, True) for b in range(2, B)]
    norms += [(BATCH_STEPS * (b + 1) + 36, 2, b, 4, True) for b in range(B - 1)]
    norms += [(BATCH_STEPS * B + 28, 2, B - 1, 2, False)]
    norms.sort()
    norm_n = {(which, b): n for n, (_, which, b, _, _) in enumerate(norms)}

    with ExitStack() as ctx:
        def sb(name, shape, dt, stack=ctx, side=None):
            return stack.enter_context(nc.sbuf_tensor(name, shape, dt, side=side))

        def sem(name):
            return ctx.enter_context(nc.semaphore(name))

        q_d = nc.dram_tensor("q_stacks", [B, H, len(Q_PART), DH, S], BF16, kind="Internal").ap()
        k_d = nc.dram_tensor("k_parts", [B, H, 3, DH, S], BF16, kind="Internal").ap()
        xn2_d = nc.dram_tensor("xn2_rows", [T, D], F32, kind="Internal").ap()

        ps_s = [ctx.enter_context(nc.psum_tensor(f"ps_s{i}", [P, 512], F32)) for i in range(3)]
        ps_t = [ctx.enter_context(nc.psum_tensor(f"ps_t{i}", [P, 512], F32)) for i in range(3)]
        ps_u = ctx.enter_context(nc.psum_tensor("ps_u", [P, 512], F32))
        ps_m = ctx.enter_context(nc.psum_tensor("ps_m", [P, 512], F32))

        ident = sb("ident", [P, P], F32)
        logits = sb("logits", [P, NT, E], F32)
        x1 = sb("x1", [P, NT, D], F32)
        same_e = sb("same_e", [P, P], F32)
        earlier = sb("earlier", [P, P], F32)
        slot_row = sb("slot_row", [P, C], BF16)
        att = ExitStack()
        late = ExitStack()
        ctx.enter_context(late)
        ctx.enter_context(att)
        xn2T = sb("xn2T", [P, DC, T], F32, late, "right")
        proj = ExitStack()
        ctx.enter_context(proj)
        wo = sb("w_o", [P, DC, D], F32, proj, "right")
        gate = sb("gate", [P, DC, E], F32, proj, "right")
        bo_b = sb("bo_b", [P, D], F32, proj, "right")
        half = sb("half", [P, QT], F32, proj, "right")
        xn = sb("xn", [P, QT, D], F32, proj, "right")
        stats = sb("stats", [P, QT, 6], F32, proj, "right")
        mv = sb("mv", [P, QT, 2], F32, proj, "right")
        rs = sb("rs", [P, 3, QT], F32, proj, "right")
        us = sb("us", [P, S], F32, proj, "right")
        rc = sb("rc", [P, QT, 4], F32, proj, "right")
        o_sb = sb("o_sb", [P, QT, D], F32, proj, "right")
        attnT = sb("attnT", [P, DC, S], F32, proj, "right")
        ctx_sb = sb("ctx_sb", [P, DC, S], F32, att)
        mk = [sb(f"mk{i}", [P, S], F32, att) for i in range(2)]
        am = [sb(f"am{i}", [P, QT, S], F32, att) for i in range(2)]
        wq, wk, wv = [sb(f"w_{n}", [P, DC, D], F32, att) for n in "qkv"]
        bqk = sb("bqk", [P, 2, DC], F32, att)
        bv_b = sb("bv_b", [P, D], F32, att)
        xlnT = sb("xlnT", [P, DC, S], F32, att)
        q32 = [sb(f"q32_{i}", [P, S], F32, att) for i in range(2)]
        parts = [sb(f"parts{i}", [P, 3, S], BF16, att) for i in range(2)]
        qs = [sb(f"qs{i}", [96, 4, S], BF16, att) for i in range(QK_RING)]
        ks = [sb(f"ks{i}", [96, 4, S], BF16, att) for i in range(QK_RING)]
        va = [sb(f"va{i}", [P, QT, H, 32], F32, att) for i in range(2)]
        sp = [sb(f"sp{i}", [P, S], F32, att) for i in range(SP_RING)]
        mn = sb("mn", [P, SP_RING], F32, att)
        pt = [sb(f"pt{i}", [P, S], F32, att) for i in range(PT_RING)]

        att.close()

        NSEG = NT // 2
        IC = I // P
        PIECES = 6
        PIECE = DC * I // 2
        BY_DVE = (0, 1, 3)
        BY_POOL = (2, 5)
        probs = sb("probs", [P, 2, NSEG, E], F32)
        soft = sb("soft", [P, NT, E], F32)
        soft1 = sb("soft1", [P, 3, NT], F32)
        ptok = sb("ptok", [P, 2 * P], F32)
        zeros = sb("zeros", [P, 2 * P], F32)
        above = sb("above", [P, 2 * P], F32)
        tied = sb("tied", [P, 2 * P], F32)
        prefix = sb("prefix", [P, 2 * P], F32)
        chosen = sb("chosen", [P, 2 * P], F32)
        bit = sb("bit", [P, 3], I32)
        theta = sb("theta", [P, 4], F32)
        cand = sb("cand", [P, 3], F32)
        cnt = sb("cnt", [P, 4], F32)
        tok_int = sb("tok_int", [P, 2, NSEG, E], I32)
        rank = sb("rank", [P, NT, E], F32)
        route = sb("route", [P, NT, E, 5], BF16)
        rank_e = [sb(f"rank_e{i}", [P, NT, 1], F32) for i in range(2)]
        route_e = [sb(f"route_e{i}", [P, NT, 5], BF16) for i in range(2)]
        wres = sb("wres", [P, NT * E], F32)
        hot = [sb("hot0", [P, NT, C], BF16)]
        rt = sb("rt", [P, 2, 5], F32)
        idx = [sb(f"idx{i}", [P, 2], U32) for i in range(2)]
        wt = [sb(f"wt{i}", [P, 2, 2], F32) for i in range(2)]
        xg = [sb(f"xg{i}", [P, 2, D], F32) for i in range(2)]
        x_hi0, x_lo0 = sb("x_hi0", [P, DC, C], F32R), sb("x_lo0", [P, DC, C], F32R)
        raw = [sb(f"raw{j}", [P, PIECE], F32) for j in range(PIECES)]
        w_hi = [[sb(f"w_hi0_{j}", [P, PIECE], F32R) for j in range(PIECES)]]
        w_lo = [[sb(f"w_lo0_{j}", [P, PIECE], F32R) for j in range(PIECES - 2)]]
        with ExitStack() as shr:
            sw_raw = [sb(f"sw_raw{j}", [P, DC * IS], F32, shr) for j in range(3)]
        shr = ExitStack()
        ctx.enter_context(shr)
        sw_lo = [sb(f"sw_lo{j}", [P, DC * IS], F32R, shr) for j in range(3)]
        sw_hi = [sb(f"sw_hi{j}", [P, DC * IS], F32R, shr) for j in range(3)]
        sh_hi = sb("sh_hi", [P, IS // P, S], F32R, shr)
        sh_lo = sb("sh_lo", [P, IS // P, S], F32R, shr)
        sx_hi = [sb(f"sx_hi{i}", [P, DC, S], F32R, shr) for i in range(2)]
        sgl = [sb(f"sgl{i}", [P, S], F32, shr) for i in range(2)]
        shid = [sb(f"shid{i}", [P, S], F32, shr) for i in range(2)]
        proj.close()
        late.close()
        sx_lo = sb("sx_lo", [P, DC, T], F32R, shr, "right")
        shr.close()
        hot.append(sb("hot1", [P, NT, C], BF16, side="right"))
        w_hi.append([sb(f"w_hi1_{j}", [P, PIECE], F32R) for j in range(PIECES)])
        w_lo.append([sb(f"w_lo1_{j}", [P, PIECE], F32R) for j in range(PIECES - 2)])
        for i in range(2):
            w_lo[i] += [sb(f"w_lo{i}_{j}", [P, PIECE], F32R, side="right") for j in range(PIECES - 2, PIECES)]
        x_hi = [x_hi0, sb("x_hi1", [P, DC, C], F32R, side="right")]
        x_lo = [x_lo0, sb("x_lo1", [P, DC, C], F32R, side="right")]
        gl = [sb(f"gl{i}", [P, C], F32, side="right") for i in range(2)]
        hid = [sb(f"hid{i}", [P, C], F32, side="right") for i in range(2)]
        h_hi = sb("h_hi", [P, IC, C], F32R, side="right")
        h_lo = sb("h_lo", [P, IC, C], F32R, side="right")
        eo = [sb(f"eo{i}", [P, 2, D], F32, side="right") for i in range(2)]

        slots = []
        for n in range(4 * B):
            slots.append(("up", n // 4, n % 4))
            if n % 4 < 2 and n >= 4:
                slots.append(("dn", n // 4 - 1, 2 * (n % 4)))
        slots += [("dn", B - 1, 0), ("dn", B - 1, 2)]
        ROUNDS = 15
        AHEAD = [UNITS + 29, UNITS + 36]

        s_top = sem("topk_chain")
        s_softin = sem("logits_shifted")
        s_softex = sem("logits_exp")
        s_probs = sem("probs_ready")
        s_ptokT = sem("probs_turned")
        s_cnt = sem("local_counts")
        s_tot = sem("total_counts")
        s_const = sem("topk_constants")
        s_pos = sem("slots_ready")
        s_posT = sem("slots_turned")
        s_route = sem("route_table")
        s_col = sem("expert_columns")
        s_hot = sem("one_hot_ready")
        s_ri = sem("routed")
        s_rt = sem("routes_chain")
        s_idx = sem("indices_ready")
        s_gath = [sem(f"gathered{i}") for i in range(2)]
        s_xgt = sem("gathered_turned")
        s_xgc = sem("gathered_copied")
        s_raw = [sem(f"piece_in{j}") for j in range(PIECES)]
        s_whi = sem("piece_high_parts")
        s_wlo = {False: sem("piece_low_by_dve"), True: sem("piece_low_by_pool")}
        s_hid = sem("hidden_float32")
        s_hhi = sem("hidden_high_part")
        s_xlo = sem("gathered_low_part")
        s_gu = sem("gate_up_ready")
        s_gl = sem("gelu_ready")
        s_h = sem("hidden_ready")
        s_dn = sem("down_ready")
        s_eo = sem("expert_out_ready")
        s_scat = sem("scattered")

        ps_i, ps_c, ps_d, ps_x = ps_s[0], ps_s[1], ps_s[2], ps_m
        ps_g = [ps_t[0], ps_t[1], ps_t[2], ps_u]

        def low_parts(eng, e, j):
            pool_n = sum(i <= j for i in BY_POOL)
            if j + 1 - pool_n:
                eng.wait_ge(s_wlo[False], (PIECES - len(BY_POOL)) * e + j + 1 - pool_n)
            if pool_n:
                eng.wait_ge(s_wlo[True], len(BY_POOL) * e + pool_n)

        def low_part(eng, e, k, j):
            eng.wait_ge(s_whi, PIECES * e + j + 1)
            eng.tensor_tensor(w_lo[k][j][:, :], raw[j][:, :], w_hi[k][j][:, :].bitcast(F32), ALU.subtract).then_inc(s_wlo[j in BY_POOL], 1)

        def bank_up(m):
            return ps_g[m % len(ps_g)]

        def ps_g_of(k, i):
            return ps_g[(IC * k + i) % len(ps_g)]

        def experts(eng, body):
            for k in range(2):
                body(k, k, 0, False)
            with eng.Fori(1, E // 2 - 1) as p:
                for k in range(2):
                    body(2 * p + k, k, p, False)
            for k in range(2):
                body(E - 2 + k, k, E // 2 - 1, True)

        s_swin = sem("shared_weights_in")
        s_sw = sem("shared_weights_high")
        s_swlo = sem("shared_up_weights_low")
        s_swdlo = sem("shared_down_weight_low")
        s_sxhi = sem("shared_x_high")
        s_sxlo = sem("shared_x_low")
        s_up = sem("shared_gate_or_up_ready")
        s_sgl = sem("shared_gelu_ready")
        s_shid = sem("shared_hidden_float32")
        s_shhi = sem("shared_hidden_high")
        s_shlo = sem("shared_hidden_low")
        s_sdn = sem("shared_down_ready")
        s_sadd = sem("shared_added")
        s_x = [sem(f"x_in{b}") for b in range(B)]
        s_cin = sem("ctx_in")
        s_mask = [sem(f"mask_in{i}") for i in range(2)]
        s_adj = sem("adj_in")
        s_w = sem("attn_weights_in")
        s_wv = sem("value_weights_in")
        s_ws = sem("output_weights_in")
        s_ident = sem("ident_ready")
        s_setup = sem("setup_done")
        s_pool = sem("pool_chain")
        s_dve = sem("dve_chain")
        s_bn = sem("tile_stats_ready")
        s_stat = sem("stats_ready")
        s_rstd = sem("rstd_ready")
        s_xn = sem("normed_ready")
        s_am = sem("am_ready")
        s_xb = sem("x_plus_bias")
        s_parts0 = sem("first_parts_ready")
        s_parts = sem("parts_ready")
        s_stored = [sem(f"parts_stored{i}") for i in range(2)]
        s_qkin = [sem(f"qk_in{i}") for i in range(QK_RING)]
        s_score = sem("score_ready")
        s_added = sem("masked_scores_ready")
        s_exp = sem("exp_ready")
        s_tr = sem("transposes_ready")
        s_eva = sem("pt_by_act")
        s_evd = sem("pt_by_dve")
        s_pv = sem("pv_ready")
        s_us = sem("us_ready")
        s_m = sem("job_filled")
        s_done = {"act": sem("job_emptied_by_act"), "dve": sem("job_emptied_by_dve")}
        s_xst = sem("xn2_stored")
        s_out = sem("out_stored")

        def by_act(s):
            return s % 16 not in BY_VECTOR

        act_before = [0]
        for s in range(LAG, UNITS + LAG):
            act_before.append(act_before[-1] + by_act(s))

        def products_of(n):
            return 4 * (n // 16) + n % 4 + 1

        def wait_moved(eng, s):
            n = s - LAG + 1
            if act_before[n]:
                eng.wait_ge(s_eva, act_before[n])
            if n - act_before[n]:
                eng.wait_ge(s_evd, n - act_before[n])

        def wait_job(eng, *key):
            j = job[key]
            eng.wait_ge(s_done[j.engine], j.done)

        def parts_made(eng, n):
            eng.wait_ge(*((s_parts0, n + 1) if n < 2 else (s_parts, n - 1)))

        def bank(j):
            return (ps_m, ps_s[0], ps_s[1])[j.bank]

        block = ctx.enter_context(nc.Block())

        @block.sync
        def _(sp):
            def load_x(b):
                sp.dma_start(x1[:, QT * b:QT * b + QT, :], x_v[:, QT * b:QT * b + QT, :]).then_inc(s_x[b], 16)

            def load_ctx(b):
                if b:
                    wait_job(sp, "v", b - 1, 3)
                sp.dma_start(ctx_sb[:, :, :], ctxT.rearrange("(c p) t -> p c t", p=P)[:, :, S * b:S * b + S]).then_inc(s_cin, 16)

            def load_adj(b):
                if b >= 2:
                    sp.wait_ge(s_added, BATCH_STEPS * (b - 1))
                sp.dma_start(am[b % 2][:, :, :], adj.rearrange("(n p) k -> p n k", p=P)).then_inc(s_adj, 16)

            def load_mask(b, qt):
                n = QT * b + qt
                if n >= 2:
                    sp.wait_ge(s_am, n - 1)
                sp.dma_start(mk[n % 2][:, :].bitcast(I32), mask[b, P * qt:P * qt + P, :]).then_inc(s_mask[n % 2], 16)

            def store_parts(b, k):
                n = 4 * b + k
                c, which = k // 2, k % 2
                parts_made(sp, n)
                HP = P // DH
                dst, kinds = (k_d, range(3)) if which else (q_d, Q_PART)
                for i, kind in enumerate(kinds):
                    sp.dma_start(dst[b, HP * c:HP * c + HP, i], parts[n % 2][:, kind, :]).then_inc(s_stored[n % 2], 16)

            def load_qk(G):
                b, g = G // 4, G % 4
                for i in range(2):
                    sp.wait_ge(s_stored[i], 16 * STORES[i] * (2 * b + g // 2 + 1))
                if G >= QK_RING:
                    sp.wait_ge(s_score, 16 * (G - QK_RING + 1))
                sp.dma_start(qs[G % QK_RING][:, :, :], q_d[b, 4 * g:4 * g + 4].rearrange("h k d t -> (k d) h t")).then_inc(s_qkin[G % QK_RING], 16)
                for lo, hi in PAIR_RUNS:
                    src = k_d[b, 4 * g:4 * g + 4, 0:hi - lo].rearrange("h k d t -> (k d) h t")
                    sp.dma_start(ks[G % QK_RING][DH * lo:DH * hi, :, :], src).then_inc(s_qkin[G % QK_RING], 16)

            load_x(0)
            load_ctx(0)
            for t, src in ((wq, WqT), (wk, WkT)):
                sp.dma_start(t[:, :, :], src.rearrange("(c p) f -> p c f", p=P)).then_inc(s_w, 16)
            for i, src in enumerate((bq, bk)):
                sp.dma_start(bqk[:, i, :], src.rearrange("(c p) -> p c", p=P), allow_slow_non_contiguous=True).then_inc(s_w, 16)
            sp.dma_start(wv[:, :, :], WvT.rearrange("(c p) f -> p c f", p=P)).then_inc(s_wv, 16)
            sp.dma_start(bv_b[:, :], bv.rearrange("(a f) -> a f", a=1).to_broadcast([P, D])).then_inc(s_wv, 16)
            load_adj(0)
            for qt in range(2):
                load_mask(0, qt)
            load_x(1)
            load_mask(0, 2)
            for s in range(FIRST, LAST):
                if s == UNITS + 20:
                    sp.wait_ge(s_us, 4 * B)
                    for t, src in zip(sw_raw, (SgT, SuT, SdT)):
                        src = src.rearrange("(c p) f -> p c f", p=P)
                        sp.dma_start(t[:, :].rearrange("p (c f) -> p c f", f=src.shape[2]), src).then_inc(s_swin, 16)
                if s == -1:
                    store_parts(0, 0)
                    load_mask(0, 3)
                    store_parts(0, 1)
                    for G in range(2):
                        load_qk(G)
                    for k in range(2, 4):
                        store_parts(0, k)
                    load_qk(2)
                    sp.dma_start(bo_b[:, :], bo.rearrange("(a f) -> a f", a=1).to_broadcast([P, D])).then_inc(s_ws, 16)
                    sp.dma_start(wo[:, :, :], WoT.rearrange("(c p) f -> p c f", p=P)).then_inc(s_ws, 16)
                    sp.dma_start(gate[:, :, :], gateT.rearrange("(c p) f -> p c f", p=P)).then_inc(s_ws, 16)
                b, r = s // BATCH_STEPS + 1, s % BATCH_STEPS
                store_at = (17, 21, 44, 48) if b > 1 else (28, 32, 44, 48)
                if 0 < b < B:
                    if r == 1:
                        load_ctx(b)
                    if r == 10 and b + 1 < B:
                        load_x(b + 1)
                    if r == 2:
                        load_adj(b)
                    if r in (2, 3, 26, 31):
                        load_mask(b, (2, 3, 26, 31).index(r))
                    if r in store_at:
                        store_parts(b, store_at.index(r))
                if (s + 28) % 16 == 0 and QK_RING <= (s + 28) // 16 < 4 * B:
                    load_qk((s + 28) // 16)
                b = s // BATCH_STEPS - 1
                if b >= 0 and s % BATCH_STEPS == (31 if b == B - 1 else 44):
                    sp.wait_ge(s_xn, norm_n[2, b] + 1)
                    sp.dma_start(xn2_d.rearrange("(n p) d -> p n d", p=P)[:, QT * b:QT * b + QT, :], xn[:, :, :]).then_inc(s_xst, 16)

            def load(e, j):
                if j < 4:
                    src = (WgT, WuT)[j % 2][e].rearrange("(c p) i -> p c i", p=P)[:, :, I // 2 * (j // 2):I // 2 * (j // 2) + I // 2]
                    dst = raw[j][:, :].rearrange("p (c i) -> p c i", c=DC)
                else:
                    src = WdT[e].rearrange("(c p) d -> p c d", p=P)[:, IC // 2 * (j - 4):IC // 2 * (j - 4) + IC // 2, :]
                    dst = raw[j][:, :].rearrange("p (c d) -> p c d", d=D)
                sp.dma_start(dst, src).then_inc(s_raw[j], 16)

            def body(e, k, p, last):
                if not last:
                    for j in range(PIECES):
                        low_parts(sp, e + 1, j)
                        load(e + 2, j)

            sp.wait_ge(s_us, 4 * B)
            for j in range(PIECES):
                load(0, j)
            for b in range(B):
                sp.wait_ge(s_sadd, QT * (b + 1))
                sp.dma_start(out_v[:, QT * b:QT * b + QT, :], x1[:, QT * b:QT * b + QT, :]).then_inc(s_out, 16)
            for j in range(PIECES):
                low_parts(sp, 0, j)
                load(1, j)
            for e in range(E):
                body(e, e % 2, e // 2, e >= E - 2)

        @block.gpsimd
        def _(pool):
            chain = [0]

            def link(ins):
                chain[0] += 1
                ins.then_inc(s_pool, 1)
                pool.wait_ge(s_pool, chain[0])

            link(pool.memset(ident[:, :], 0.0))
            pool.affine_select(out=ident[:, :], in_=ident[:, :], compare_op=ALU.not_equal, fill=1.0,
                               base=0, pattern=[[-1, P]], channel_multiplier=1).then_inc(s_ident, 1)
            pool.memset(half[:, :], -0.5).then_inc(s_setup, 1)
            for i in range(2):
                link(pool.memset(va[i][:, :, :, DH:32], 0.0))
                pool.memset(va[i][:, :, :, DH:DH + 1], 1.0).then_inc(s_setup, 1)
            pool.wait_ge(s_setup, 3)

            def rstd(n):
                pool.wait_ge(s_stat, n + 1)
                link(pool.tensor_scalar(rs[:, 1, :], mv[:, :, 1], EPS, None, ALU.add))
                link(pool.tensor_tensor(rs[:, 0, :], rs[:, 1, :], half[:, :], ALU.pow))
                link(pool.tensor_tensor(rs[:, 2, :], rs[:, 0, :], rs[:, 0, :], ALU.mult))
                link(pool.tensor_tensor(rs[:, 2, :], rs[:, 2, :], rs[:, 1, :], ALU.mult))
                link(pool.tensor_scalar(rs[:, 2, :], rs[:, 2, :], -0.5, 1.5, ALU.mult, ALU.add))
                pool.tensor_tensor(rs[:, 0, :], rs[:, 0, :], rs[:, 2, :], ALU.mult).then_inc(s_rstd, 1)

            def split(b, k):
                n = 4 * b + k
                wait_job(pool, "qk"[k % 2], b, k // 2)
                if n >= 2:
                    pool.wait_ge(s_stored[n % 2], 16 * STORES[n % 2] * (n // 2))
                q, p = q32[n % 2], parts[n % 2]
                link(pool.tensor_copy(p[:, 0, :], q[:, :]))
                link(pool.tensor_tensor(q[:, :], q[:, :], p[:, 0, :], ALU.subtract))
                link(pool.tensor_copy(p[:, 1, :], q[:, :]))
                pool.tensor_tensor(p[:, 2, :], q[:, :], p[:, 1, :], ALU.subtract).then_inc(s_parts, 1)

            def build_am(b, qt):
                n = QT * b + qt
                pool.wait_ge(s_mask[n % 2], 16 * (n // 2 + 1))
                if qt == 0:
                    pool.wait_ge(s_adj, 16 * (b + 1))
                m, a = mk[n % 2], am[b % 2][:, qt, :]
                link(pool.tensor_scalar(m[:, :], m[:, :].bitcast(I32), 0.0, MASKED, ALU.is_equal, ALU.mult))
                pool.tensor_tensor(a, m[:, :], a, ALU.subtract).then_inc(s_am, 1)

            def add_bias(b):
                if b == 0:
                    pool.wait_ge(s_ws, 16 * 3)
                pool.wait_ge(s_xn, norm_n[1, b] + 1)
                for t in range(QT * b, QT * b + QT):
                    i = pool.tensor_tensor(x1[:, t, :], x1[:, t, :], bo_b[:, :], ALU.add)
                i.then_inc(s_xb, 1)

            def shared_low(n):
                pool.wait_ge(s_shhi, n + 1)
                if n >= 4 and n % 4 == 0:
                    pool.wait_ge(s_sdn, n)
                pool.tensor_tensor(sh_lo[:, n % 4, :], shid[n % 2][:, :], sh_hi[:, n % 4, :].bitcast(F32), ALU.subtract).then_inc(s_shlo, 1)

            def shared_x_low(b):
                pool.wait_ge(s_sxhi, b + 1)
                x = xn2T[:, :, S * b:S * b + S]
                pool.tensor_tensor(sx_lo[:, :, S * b:S * b + S], x, sx_hi[b % 2][:, :, :].bitcast(F32), ALU.subtract).then_inc(s_sxlo, 1)

            lowered = [0]

            def low_slot():
                kind, b, i = slots[lowered[0]]
                lowered[0] += 1
                if kind == "up":
                    shared_low(4 * b + i)
                    if i == 1 and b + 1 < B:
                        shared_x_low(b + 1)
                    if b == 2 and i == 2:
                        low_part(pool, 0, 0, 2)

            for s in range(FIRST, LAST):
                for n, (at, which, b, _, _) in enumerate(norms):
                    if at == s:
                        rstd(n)
                if s == UNITS + 25:
                    pool.wait_ge(s_us, 4 * B)
                    link(pool.iota(tok_int[:, :, :, :], [[P, 2], [2 * P, NSEG], [0, E]], base=0, channel_multiplier=0))
                    link(pool.tensor_copy(route[:, :, :, 0], tok_int[:, :, :, :].rearrange("p h s e -> p (h s) e")))
                    link(pool.iota(tok_int[:, :, :, :], [[0, 2], [0, NSEG], [0, E]], base=0, channel_multiplier=1))
                    link(pool.tensor_copy(route[:, :, :, 1], tok_int[:, :, :, :].rearrange("p h s e -> p (h s) e")))
                    pool.memset(zeros[:, :], 0.0).then_inc(s_const, 1)
                    shared_x_low(0)
                if s == UNITS + 30:
                    pool.wait_ge(s_sw, 3)
                    pool.tensor_tensor(sw_lo[2][:, :], sw_raw[2][:, :], sw_hi[2][:, :].bitcast(F32), ALU.subtract).then_inc(s_swdlo, 1)
                b, r = s // BATCH_STEPS + 1, s % BATCH_STEPS
                split_at = (12, 15, 38, 42) if b > 1 else (23, 27, 38, 42)
                if s == BATCH_STEPS * (B - 1) + 8:
                    for c in range(0, C, P):
                        link(pool.iota(earlier[:, :].bitcast(I32), [[1, P]], base=c + 1, channel_multiplier=0))
                        link(pool.tensor_copy(slot_row[:, c:c + P], earlier[:, :].bitcast(I32)))
                    link(pool.memset(same_e[:, :], 0.0))
                    for m in range(1 - NSEG, NSEG):
                        link(pool.affine_select(out=same_e[:, :], in_=same_e[:, :], compare_op=ALU.not_equal, fill=1.0,
                                                base=-E * m, pattern=[[-1, P]], channel_multiplier=1))
                    link(pool.affine_select(out=earlier[:, :], in_=same_e[:, :], compare_op=ALU.is_gt, fill=0.0,
                                            base=0, pattern=[[1, P]], channel_multiplier=-1))
                if s == -1:
                    for qt in range(QT):
                        build_am(0, qt)
                    for k in range(2, 4):
                        split(0, k)
                if s == 20:
                    add_bias(0)
                if 0 < b < B:
                    if r in split_at:
                        split(b, split_at.index(r))
                    if r in (24, 28, 46, 50):
                        build_am(b, (24, 28, 46, 50).index(r))
                    if r == 32:
                        add_bias(b)

            while lowered[0] < len(slots):
                low_slot()

            def gather(e, k):
                pool.wait_ge(s_idx, e + 1)
                pool.wait_ge(s_xst, 16 * B)
                for ch in range(2):
                    pool.indirect_dma_start(out=xg[k][:, ch, :], out_offset=None, in_=xn2_d,
                                            in_offset=bass.IndirectOffsetOnAxis(ap=idx[k][:, ch:ch + 1], axis=0)).then_inc(s_gath[k], 16)

            def scatter(e, k):
                pool.wait_ge(s_eo, e + 1)
                if not isinstance(e, int) or e:
                    pool.wait_ge(s_scat, 32 * e)
                pool.wait_ge(s_out, 16 * B)
                for ch in range(2):
                    pool.indirect_dma_start(out=out, out_offset=bass.IndirectOffsetOnAxis(ap=idx[k][:, ch:ch + 1], axis=0),
                                            in_=eo[k][:, ch, :], in_offset=None,
                                            compute_op=ALU.add).then_inc(s_scat, 16)

            def body(e, k, p, last):
                if not last:
                    gather(e + 1, 1 - k)
                    for j in BY_POOL:
                        low_part(pool, e + 1, 1 - k, j)
                scatter(e, k)

            gather(0, 0)
            low_part(pool, 0, 0, 5)
            for e in range(E):
                body(e, e % 2, e // 2, e == E - 1)
            pool.wait_ge(s_scat, 32 * E)

        @block.scalar
        def _(act):
            def exp(u):
                act.wait_ge(s_added, u + 1)
                act.activation(sp[u % SP_RING][:, :], sp[u % SP_RING][:, :], ACT.Exp, bias=mn[:, u % SP_RING:u % SP_RING + 1], scale=-1.0).then_inc(s_exp, 1)

            def move_pt(s):
                act.wait_ge(s_tr, s - LAG + 1)
                n = s - LAG
                if n >= PT_RING:
                    act.wait_ge(s_pv, products_of(n - PT_RING))
                act.activation(pt[n % PT_RING][:, :], ps_t[s % 3][:, :], ACT.Copy).then_inc(s_eva, 1)

            def empty(j):
                act.wait_ge(s_m, j.n + 1)
                m = bank(j)
                if j.kind == "xT":
                    if j.b:
                        wait_job(act, "k", j.b - 1, 1)
                    i = act.activation(xlnT[:, j.i, :], m[:, :], ACT.Copy)
                if j.kind == "aT":
                    if j.b:
                        wait_job(act, "y", j.b - 1, 3)
                    i = act.activation(attnT[:, j.i, :], m[:, :], ACT.Copy)
                if j.kind == "xn2T":
                    i = act.activation(xn2T[:, j.i, S * j.b:S * j.b + S], m[:, :], ACT.Copy)
                i.then_inc(s_done["act"], 1)

            def high_part(e, k, j):
                act.wait_ge(s_raw[j], 16 * (e + 1))
                if isinstance(e, int) and e == 1:
                    act.wait_ge(s_sdn, NT)
                if not isinstance(e, int) or e >= 2:
                    if j < 4:
                        act.wait_ge(s_gu, IC * (e - 2) + (4 if j < 2 else 8))
                    else:
                        act.wait_ge(s_dn, e - 1)
                act.activation(w_hi[k][j][:, :], raw[j][:, :], ACT.Copy).then_inc(s_whi, 1)

            def shared_x_high(b):
                if b >= 2:
                    act.wait_ge(s_up, 8 * (b - 1))
                act.activation(sx_hi[b % 2][:, :, :], xn2T[:, :, S * b:S * b + S], ACT.Copy).then_inc(s_sxhi, 1)

            def shared_hidden_high(n):
                act.wait_ge(s_shid, n + 1)
                if n >= 4 and n % 4 == 0:
                    act.wait_ge(s_sdn, n)
                act.activation(sh_hi[:, n % 4, :], shid[n % 2][:, :], ACT.Copy).then_inc(s_shhi, 1)

            def split_shared_weights():
                shared_x_high(0)
                act.wait_ge(s_swin, 16 * 3)
                for j in range(3):
                    act.activation(sw_hi[j][:, :], sw_raw[j][:, :], ACT.Copy).then_inc(s_sw, 1)

            taken = [0]

            def gelu_slot():
                kind, b, i = slots[taken[0]]
                taken[0] += 1
                n = 4 * b + i
                if kind == "up":
                    act.wait_ge(s_up, 2 * n + 1)
                    if n >= 2:
                        act.wait_ge(s_shid, n - 1)
                    act.activation(sgl[n % 2][:, :], bank_up(2 * n)[:, :], ACT.Gelu).then_inc(s_sgl, 1)
                    if n:
                        shared_hidden_high(n - 1)
                    if i == 0 and b + 1 < B:
                        shared_x_high(b + 1)
                    if 4 < n < 5 + PIECES:
                        high_part(0, 0, n - 5)
                    if n == 4 * B - 1:
                        shared_hidden_high(n)

            for s in range(FIRST, LAST):
                if 0 <= s - 1 < UNITS:
                    exp(s - 1)
                if LAG <= s - 1 < UNITS + LAG and by_act(s - 1):
                    move_pt(s - 1)
                G = (s - PV_AT - 1) // 16 - 1
                if (s - PV_AT) % 16 == 3 * PV_EVERY + 1 and 0 <= G < 4 * B:
                    act.wait_ge(s_pv, 4 * (G + 1))
                    if G:
                        act.wait_ge(s_m, job["norm", (G - 1) // 4, (G - 1) % 4].n + 1)
                    act.activation(us[:, :], ps_u[:, :], ACT.Copy).then_inc(s_us, 1)
                for j in jobs:
                    if j.step == s - 1 and j.engine == "act":
                        empty(j)
                if s == UNITS + 23:
                    split_shared_weights()

            act.wait_ge(s_softin, 1)
            act.activation(soft[:, :, :], soft[:, :, :], ACT.Exp).then_inc(s_softex, 1)

            def copy_gathered(e, k):
                act.wait_ge(s_xgt, e + 1)
                if not isinstance(e, int) or e >= 2:
                    act.wait_ge(s_gu, IC * (e - 1))
                act.activation(x_hi[k][:, :, :], ps_x[:, :].rearrange("p (c t) -> p c t", c=DC), ACT.Copy).then_inc(s_xgc, 1)

            def hidden_high(e, i):
                act.wait_ge(s_hid, IC * e + i + 1)
                if i == 0 and (not isinstance(e, int) or e):
                    act.wait_ge(s_dn, e)
                act.activation(h_hi[:, i, :], hid[i % 2][:, :], ACT.Copy).then_inc(s_hhi, 1)

            def body(e, k, p, last):
                for i in range(IC):
                    act.wait_ge(s_gu, IC * e + i + 1)
                    if not isinstance(p, int) or p or k or i >= 2:
                        act.wait_ge(s_hid, IC * e + i - 1)
                    act.activation(gl[i % 2][:, :], ps_g_of(k, i)[:, 0:C], ACT.Gelu).then_inc(s_gl, 1)
                    if i:
                        hidden_high(e, i - 1)
                    if i < PIECES and not (last and k == 1):
                        high_part(e + 1, 1 - k, i)
                hidden_high(e, IC - 1)
                if not (last and k == 1):
                    copy_gathered(e + 1, 1 - k)

            while taken[0] < len(slots):
                gelu_slot()
            copy_gathered(0, 0)
            experts(act, body)

        @block.vector
        def _(dve):
            chain = [0]

            def link(ins):
                chain[0] += 1
                ins.then_inc(s_dve, 1)
                dve.wait_ge(s_dve, chain[0])

            def add_mask(u):
                b, qt = u // BATCH_STEPS, u % 4
                dve.wait_ge(s_score, u + 1)
                if u % BATCH_STEPS < QT:
                    dve.wait_ge(s_am, QT * b + qt + 1)
                if u >= SP_RING:
                    dve.wait_ge(s_tr, 4 * ((u - SP_RING) // 4 + 1))
                dve.tensor_tensor_reduce(sp[u % SP_RING][:, :], ps_s[u % 3][:, :], am[b % 2][:, qt, :], 1.0, LARGEST,
                                         ALU.add, ALU.min, mn[:, u % SP_RING:u % SP_RING + 1]).then_inc(s_added, 1)

            def move_pt(s):
                dve.wait_ge(s_tr, s - LAG + 1)
                n = s - LAG
                if n >= PT_RING:
                    dve.wait_ge(s_pv, products_of(n - PT_RING))
                dve.tensor_copy(pt[n % PT_RING][:, :], ps_t[s % 3][:, :]).then_inc(s_evd, 1)

            def statistics(n, b, t):
                if n:
                    dve.wait_ge(s_xn, n)
                dve.bn_stats(stats[:, t, :], x1[:, QT * b + t, :]).then_inc(s_bn, 1)

            def aggregate(n):
                dve.wait_ge(s_bn, QT * (n + 1))
                for t in range(QT):
                    i = dve.bn_aggr(mv[:, t, :], stats[:, t, :])
                i.then_inc(s_stat, 1)

            def apply(n, b, t):
                if t == 0:
                    dve.wait_ge(s_rstd, n + 1)
                if t == 0 and n:
                    _, w, pb, _, _ = norms[n - 1]
                    dve.wait_ge(s_m, job["xT" if w == 1 else "xn2T", pb, 1].n + 1)
                    stored = sum(norm[1] == 2 for norm in norms[:n])
                    if stored:
                        dve.wait_ge(s_xst, 16 * stored)
                i = dve.tensor_scalar(xn[:, t, :], x1[:, QT * b + t, :], mv[:, t, 0:1], rs[:, 0, t:t + 1],
                                      ALU.subtract, ALU.mult)
                if t == QT - 1:
                    i.then_inc(s_xn, 1)

            def empty(j):
                dve.wait_ge(s_m, j.n + 1)
                m, b, i = bank(j), j.b, j.i
                if j.kind in "qk":
                    k = 2 * i + (j.kind == "k")
                    n = 4 * b + k
                    if n >= 2:
                        parts_made(dve, n - 2)
                    which = int(j.kind == "k")
                    scale = -1.0 / DH ** 0.5 if j.kind == "q" else 1.0
                    last = dve.tensor_scalar(q32[n % 2][:, :], m[:, :], bqk[:, which, i:i + 1], scale, ALU.add, ALU.mult)
                if j.kind == "v":
                    if b >= 2:
                        dve.wait_ge(s_pv, 16 * (b - 1))
                    last = dve.tensor_tensor(va[b % 2][:, i, :, 0:DH], m[:, 0:D].rearrange("p (h d) -> p h d", h=H),
                                             bv_b[:, :].rearrange("p (h d) -> p h d", h=H), ALU.add)
                if j.kind == "norm":
                    mm = m[:, :].rearrange("p (q j r) -> p q j r", q=QT, r=32)
                    if b and i == 0:
                        dve.wait_ge(s_m, job["aT", b - 1, 1].n + 1)
                    if j.before_norm:
                        wait_job(dve, *j.before_norm)
                    link(dve.reciprocal(rc[:, :, :], mm[:, :, :, DH]))
                    last = dve.tensor_tensor(o_sb[:, :, 64 * i:64 * i + 64].rearrange("p q (j d) -> p q j d", d=DH),
                                             mm[:, :, :, 0:DH], rc[:, :, :].unsqueeze(3).to_broadcast([P, QT, 4, DH]), ALU.mult)
                if j.kind == "y":
                    if i == 0:
                        dve.wait_ge(s_xb, b + 1)
                    last = dve.tensor_tensor(x1[:, QT * b + i, :], m[:, 0:D], x1[:, QT * b + i, :], ALU.add)
                if j.kind == "lg":
                    last = dve.tensor_copy(logits[:, QT * b:QT * b + QT, :], m[:, 0:QT * E].rearrange("p (q e) -> p q e", e=E))
                last.then_inc(s_done["dve"], 1)
                if j.kind in "qk" and n < 2:
                    wait_job(dve, j.kind, b, i)
                    q, p = q32[n], parts[n]
                    link(dve.tensor_copy(p[:, 0, :], q[:, :]))
                    link(dve.tensor_tensor(q[:, :], q[:, :], p[:, 0, :], ALU.subtract))
                    link(dve.tensor_copy(p[:, 1, :], q[:, :]))
                    dve.tensor_tensor(p[:, 2, :], q[:, :], p[:, 1, :], ALU.subtract).then_inc(s_parts0, 1)

            def shared_empty(kind, b, i):
                n = 4 * b + i
                if kind == "up":
                    dve.wait_ge(s_up, 2 * n + 2)
                    dve.wait_ge(s_sgl, n + 1)
                    if n >= 2:
                        dve.wait_ge(s_shlo, n - 1)
                    dve.tensor_tensor(shid[n % 2][:, :], bank_up(2 * n + 1)[:, :], sgl[n % 2][:, :], ALU.mult).then_inc(s_shid, 1)
                else:
                    for qt in (i, i + 1):
                        m = QT * b + qt
                        dve.wait_ge(s_sdn, m + 1)
                        dve.tensor_tensor(x1[:, m, :], (ps_d, ps_x)[m % 2][:, 0:D], x1[:, m, :], ALU.add).then_inc(s_sadd, 1)

            emptied = [0]

            def empty_slot():
                if emptied[0] < len(slots):
                    shared_empty(*slots[emptied[0]])
                    emptied[0] += 1

            for s in range(FIRST, LAST):
                if s == -14:
                    dve.wait_ge(s_w, 16 * 4)
                    dve.wait_ge(s_wv, 16 * 2)
                    dve.wait_ge(s_setup, 3)
                if 0 <= s < UNITS:
                    add_mask(s)
                if LAG <= s - 1 < UNITS + LAG and not by_act(s - 1):
                    move_pt(s - 1)
                if s == UNITS + 29:
                    for j in range(2):
                        dve.wait_ge(s_sw, j + 1)
                        dve.tensor_tensor(sw_lo[j][:, :], sw_raw[j][:, :], sw_hi[j][:, :].bitcast(F32), ALU.subtract).then_inc(s_swlo, 1)
                for n, (at, which, b, behind, spread) in enumerate(norms):
                    for t in range(QT):
                        if s == (at - QT + t if spread else at):
                            if which == 1:
                                dve.wait_ge(s_x[b], 16)
                            else:
                                wait_job(dve, "y", b, t)
                            statistics(n, b, t)
                    if at == s:
                        aggregate(n)
                    for t in range(QT):
                        if s == at + behind + t * spread:
                            apply(n, b, t)
                for j in jobs:
                    if j.step == s - 1 and j.engine == "dve":
                        empty(j)

            top = [0]

            def then(ins):
                top[0] += 1
                ins.then_inc(s_top, 1)
                dve.wait_ge(s_top, top[0])

            dve.wait_ge(s_us, 4 * B)
            wait_job(dve, "lg", B - 1, 0)
            then(dve.tensor_reduce(soft1[:, 0, :], logits[:, :, :], AX.X, ALU.max))
            dve.tensor_tensor(soft[:, :, :], logits[:, :, :], soft1[:, 0, :].unsqueeze(2).to_broadcast([P, NT, E]), ALU.subtract).then_inc(s_softin, 1)
            dve.wait_ge(s_softex, 1)
            then(dve.tensor_reduce(soft1[:, 1, :], soft[:, :, :], AX.X, ALU.add))
            then(dve.reciprocal(soft1[:, 2, :], soft1[:, 1, :]))
            dve.tensor_tensor(probs[:, :, :, :], soft[:, :, :].rearrange("p (s h) e -> p h s e", h=2),
                              soft1[:, 2, :].rearrange("p (s h) -> p h s", h=2).unsqueeze(3).to_broadcast([P, 2, NSEG, E]), ALU.mult).then_inc(s_probs, 1)
            dve.wait_ge(s_probs, 1)
            flat = probs[:, :, :, :].rearrange("p h s e -> p (h s e)")
            flat_route = route[:, :, :, :].rearrange("p n e k -> p (n e) k")
            dve.wait_ge(s_const, 1)
            then(dve.tensor_copy(flat_route[:, :, 2], flat))
            then(dve.tensor_tensor(wres[:, :], flat, flat_route[:, :, 2], ALU.subtract))
            then(dve.tensor_copy(flat_route[:, :, 3], wres[:, :]))
            dve.tensor_tensor(flat_route[:, :, 4], wres[:, :], flat_route[:, :, 3], ALU.subtract).then_inc(s_route, 1)

            for c in range(3):
                then(dve.memset(bit[:, c:c + 1], (c + 1) << 28))
            then(dve.memset(theta[:, :], 0.0))
            dve.wait_ge(s_ptokT, 1)
            then(dve.tensor_copy(ptok[:, :], ps_i[:, 0:2 * P]))
            empty_slot()
            for n in range(ROUNDS):
                then(dve.tensor_tensor(cand[:, :].bitcast(I32), theta[:, 0:1].bitcast(I32).to_broadcast([P, 3]), bit[:, :], ALU.bitwise_or))
                for c in range(3):
                    last = dve.tensor_scalar((prefix, above, tied)[c][:, :], ptok[:, :], cand[:, c:c + 1], 0.0, ALU.is_ge, ALU.add, accum_out=cnt[:, c:c + 1])
                last.then_inc(s_cnt, 1)
                then(dve.tensor_scalar(bit[:, :], bit[:, :], 2, None, ALU.logical_shift_right))
                empty_slot()
                if n >= ROUNDS - len(BY_DVE):
                    low_part(dve, 0, 0, BY_DVE[n - ROUNDS + len(BY_DVE)])
                dve.wait_ge(s_tot, n + 1)
                then(dve.scalar_tensor_tensor(theta[:, 1:4], ps_c[:, 0:3], float(C), cand[:, :], ALU.is_ge, ALU.mult))
                then(dve.tensor_reduce(theta[:, 0:1], theta[:, 0:4], AX.X, ALU.max))
            then(dve.tensor_scalar(above[:, :], ptok[:, :], theta[:, 0:1], 0.0, ALU.is_gt, ALU.add, accum_out=cnt[:, 0:1]))
            then(dve.tensor_scalar(tied[:, :], ptok[:, :], theta[:, 0:1], 0.0, ALU.is_equal, ALU.add, accum_out=cnt[:, 1:2]))
            dve.tensor_tensor_scan(prefix[:, :], tied[:, :], zeros[:, :], 0.0, ALU.add, ALU.add).then_inc(s_cnt, 1)
            empty_slot()
            dve.wait_ge(s_tot, ROUNDS + 1)
            then(dve.tensor_copy(cnt[:, 2:4], ps_c[:, 0:2]))
            then(dve.tensor_tensor(cnt[:, 2:3], cnt[:, 2:3], cnt[:, 3:4], ALU.add))
            then(dve.tensor_scalar(cnt[:, 2:3], cnt[:, 2:3], -1.0, float(C), ALU.mult, ALU.add))
            dve.wait_ge(s_cnt, ROUNDS + 1)
            then(dve.scalar_tensor_tensor(tied[:, :], prefix[:, :], cnt[:, 2:3], tied[:, :], ALU.is_le, ALU.mult))
            dve.scalar_tensor_tensor(chosen[:, :], tied[:, :], 1.0, above[:, :], ALU.mult, ALU.add, accum_out=cnt[:, 0:1]).then_inc(s_cnt, 1)
            dve.wait_ge(s_cnt, ROUNDS + 2)
            then(dve.tensor_tensor_scan(prefix[:, :], chosen[:, :], zeros[:, :], 0.0, ALU.add, ALU.add))
            empty_slot()
            dve.wait_ge(s_tot, ROUNDS + 2)
            dve.scalar_tensor_tensor(prefix[:, :], prefix[:, :], ps_c[:, 0:1], chosen[:, :], ALU.add, ALU.mult).then_inc(s_pos, 1)
            empty_slot()
            dve.wait_ge(s_posT, 1)
            then(dve.tensor_copy(rank[:, :, :], ps_i[:, 0:2 * P].rearrange("p (n e) -> p n e", e=E)))

            def one_hot(e, k):
                if not isinstance(e, int) or e >= 2:
                    dve.wait_ge(s_ri, e - 1)
                dve.tensor_copy(rank_e[k][:, :, :], rank[:, :, bass.ds(e, 1)]).then_inc(s_col, 1)
                dve.tensor_copy(route_e[k][:, :, :], route[:, :, bass.ds(e, 1), :].rearrange("p n a k -> p n (a k)"))
                dve.wait_ge(s_col, e + 1)
                for n in range(NT):
                    i = dve.tensor_scalar(hot[k][:, n, :], slot_row[:, :], rank_e[k][:, n, :], None, ALU.is_equal)
                i.then_inc(s_hot, 1)

            def take_routes(e, k):
                dve.wait_ge(s_ri, e + 1)
                r = ps_i[:, 0:10].rearrange("p (c k) -> p c k", k=5)
                if not isinstance(e, int) or e >= 2:
                    dve.wait_ge(s_scat, 32 * (e - 1))
                dve.tensor_copy(rt[:, :, :], r).then_inc(s_rt, 1)
                dve.wait_ge(s_rt, 2 * e + 1)
                dve.tensor_tensor(idx[k][:, :], rt[:, :, 0], rt[:, :, 1], ALU.add)
                dve.tensor_tensor(wt[k][:, 0, :], rt[:, :, 2], rt[:, :, 3], ALU.add).then_inc(s_rt, 1)
                dve.wait_ge(s_rt, 2 * e + 2)
                dve.tensor_tensor(wt[k][:, 1, :], wt[k][:, 0, :], rt[:, :, 4], ALU.add).then_inc(s_idx, 1)

            def gathered_low(e, k):
                dve.wait_ge(s_xgc, e + 1)
                dve.tensor_tensor(x_lo[k][:, :, :], ps_x[:, :].rearrange("p (c t) -> p c t", c=DC),
                                  x_hi[k][:, :, :].bitcast(F32), ALU.subtract).then_inc(s_xlo, 1)

            def hidden_low(e, i):
                dve.wait_ge(s_hhi, IC * e + i + 1)
                dve.tensor_tensor(h_lo[:, i, :], hid[i % 2][:, :], h_hi[:, i, :].bitcast(F32), ALU.subtract).then_inc(s_h, 1)

            def body(e, k, p, last):
                for i in range(IC):
                    if i == 2 and not (last and k == 1):
                        take_routes(e + 1, 1 - k)
                    dve.wait_ge(s_gl, IC * e + i + 1)
                    if not isinstance(p, int) or p or k or i >= 2:
                        dve.wait_ge(s_h, IC * e + i - 1)
                    dve.tensor_tensor(hid[i % 2][:, :], ps_g_of(k, i)[:, C:2 * C], gl[i % 2][:, :], ALU.mult).then_inc(s_hid, 1)
                    if i:
                        hidden_low(e, i - 1)
                    if i < PIECES and i not in BY_POOL and not (last and k == 1):
                        low_part(dve, e + 1, 1 - k, i)
                hidden_low(e, IC - 1)
                if not (last and k == 1):
                    gathered_low(e + 1, 1 - k)
                if not last:
                    one_hot(e + 2, k)
                dve.wait_ge(s_dn, e + 1)
                dve.wait_ge(s_idx, e + 1)
                for ch in range(2):
                    i = dve.tensor_scalar(eo[k][:, ch, :], (ps_d, ps_c)[ch][:, 0:D], wt[k][:, 1, ch:ch + 1], None, ALU.mult)
                i.then_inc(s_eo, 1)

            one_hot(0, 0)
            empty_slot()
            empty_slot()
            take_routes(0, 0)
            empty_slot()
            while emptied[0] < len(slots) - 2:
                empty_slot()
            one_hot(1, 1)
            while emptied[0] < len(slots):
                empty_slot()
            gathered_low(0, 0)
            low_part(dve, 0, 0, 4)
            experts(dve, body)

        @block.tensor
        def _(pe):
            def score(u):
                G, h, qt = u // 16, (u // 4) % 4, u % 4
                if u % 16 == 0:
                    pe.wait_ge(s_qkin[G % QK_RING], 16 * 4 * (G // QK_RING + 1))
                if u >= 3:
                    pe.wait_ge(s_added, u - 2)
                pe.matmul(ps_s[u % 3][:, :], qs[G % QK_RING][:, h, P * qt:P * qt + P], ks[G % QK_RING][:, h, :],
                          start=True, stop=True).then_inc(s_score, 1)

            def transposes(s):
                h, kt = (s - LAG) // 4, (s - LAG) % 4
                if kt == 0:
                    pe.wait_ge(s_exp, 4 * h + 4)
                if s - 3 >= LAG:
                    wait_moved(pe, s - 3)
                for qt in range(QT):
                    i = pe.transpose(ps_t[s % 3][:, P * qt:P * qt + P], sp[(4 * h + qt) % SP_RING][:, P * kt:P * kt + P], ident[:, :])
                i.then_inc(s_tr, 1)

            def pv(G, kt):
                if kt == 0 and G:
                    pe.wait_ge(s_us, G)
                wait_moved(pe, 4 * (4 * G + 3) + LAG + kt)
                b, g = G // 4, G % 4
                for j in range(4):
                    i = pe.matmul(ps_u[32 * j:32 * j + 32, :], va[b % 2][:, kt, 4 * g + j, :], pt[(16 * G + 4 * j + kt) % PT_RING][:, :],
                                  start=(kt == 0), stop=(kt == 3))
                i.then_inc(s_pv, 1)

            def fill(j, s):
                m, b, i = bank(j), j.b, j.i
                if j.before and s == j.first:
                    pe.wait_ge(s_done[j.before.engine], j.before.done)
                if j.kind in ("xT", "xn2T"):
                    pe.wait_ge(s_xn, norm_n[1 if j.kind == "xT" else 2, b] + 1)
                    for t in range(QT):
                        last = pe.transpose(m[:, P * t:P * t + P], xn[:, t, P * i:P * i + P], ident[:, :])
                if j.kind in "qk":
                    wait_job(pe, "xT", b, 1)
                    pe.wait_ge(s_cin, 16 * (b + 1))
                    if b == 0 and i == 0:
                        pe.wait_ge(s_w, 16 * 4)
                    w, src = (wq, xlnT) if j.kind == "q" else (wk, ctx_sb)
                    for c in range(DC):
                        if (j.first, j.step)[c] == s:
                            last = pe.matmul(m[:, :], w[:, c, P * i:P * i + P], src[:, c, :], start=(c == 0), stop=(c == DC - 1))
                    if s < j.step:
                        return
                if j.kind == "v":
                    if b == 0 and i == 0:
                        pe.wait_ge(s_wv, 16 * 2)
                    for c in range(DC):
                        last = pe.matmul(m[:, 0:D], ctx_sb[:, c, P * i:P * i + P], wv[:, c, :], start=(c == 0), stop=(c == DC - 1))
                if j.kind == "norm":
                    pe.wait_ge(s_us, 4 * b + i + 1)
                    for t in range(QT):
                        last = pe.transpose(m[:, P * t:P * t + P], us[:, P * t:P * t + P], ident[:, :])
                if j.kind == "aT":
                    wait_job(pe, "norm", b, 3)
                    for t in range(QT):
                        last = pe.transpose(m[:, P * t:P * t + P], o_sb[:, t, P * i:P * i + P], ident[:, :])
                if j.kind == "y":
                    wait_job(pe, "aT", b, 1)
                    if b == 0 and i == 0:
                        pe.wait_ge(s_ws, 16 * 3)
                    for c in range(DC):
                        last = pe.matmul(m[:, 0:D], attnT[:, c, P * i:P * i + P], wo[:, c, :], start=(c == 0), stop=(c == DC - 1))
                if j.kind == "lg":
                    wait_job(pe, "xn2T", b, 1)
                    for t in range(QT):
                        for c in range(DC):
                            last = pe.matmul(m[:, E * t:E * t + E], xn2T[:, c, S * b + P * t:S * b + P * t + P], gate[:, c, :], start=(c == 0), stop=(c == DC - 1))
                last.then_inc(s_m, 1)

            def keep_warm(n):
                for _ in range(n):
                    pe.matmul(ps_s[2][:, 0:P], ident[:, :], ident[:, :], start=True, stop=True)

            def exact(out, a_hi, a_lo, b_hi, b_lo, start, stop):
                pe.matmul(out, a_hi, b_hi, start=start, stop=False)
                pe.matmul(out, a_hi, b_lo, start=False, stop=False)
                return pe.matmul(out, a_lo, b_hi, start=False, stop=stop)

            def shared(kind, b, i):
                if kind == "up":
                    n = 4 * b + i
                    if i == 0:
                        pe.wait_ge(s_sxlo, b + 1)
                    for which in range(2):
                        if b == 0 and i == 0:
                            pe.wait_ge(s_swlo, which + 1)
                        m = 2 * n + which
                        if m >= len(ps_g):
                            pe.wait_ge(s_shid, (m - len(ps_g)) // 2 + 1)
                        for c in range(DC):
                            at = IS * c + P * i
                            last = exact(bank_up(m)[:, :], sw_hi[which][:, at:at + P], sw_lo[which][:, at:at + P],
                                         sx_hi[b % 2][:, c, :], sx_lo[:, c, S * b:S * b + S], c == 0, c == DC - 1)
                        last.then_inc(s_up, 1)
                else:
                    if b == 0 and i == 0:
                        pe.wait_ge(s_swdlo, 1)
                    pe.wait_ge(s_shlo, 4 * (b + 1))
                    for qt in (i, i + 1):
                        m = QT * b + qt
                        if m >= 2:
                            pe.wait_ge(s_sadd, m - 1)
                        for c in range(IS // P):
                            last = exact((ps_d, ps_x)[m % 2][:, 0:D], sh_hi[:, c, P * qt:P * qt + P], sh_lo[:, c, P * qt:P * qt + P],
                                         sw_hi[2][:, D * c:D * c + D], sw_lo[2][:, D * c:D * c + D], c == 0, c == IS // P - 1)
                        last.then_inc(s_sdn, 1)

            filled = [0]

            def fill_slot():
                if filled[0] < len(slots):
                    shared(*slots[filled[0]])
                    filled[0] += 1

            pe.wait_ge(s_ident, 1)
            keep_warm(WARM["start"])
            for s in range(FIRST, LAST):
                if s == 0:
                    keep_warm(WARM["scores"])
                    pe.wait_ge(s_setup, 3)
                    wait_job(pe, "v", 0, 3)
                if s == UNITS + 27:
                    keep_warm(WARM["norm"])
                if 0 <= s < UNITS:
                    score(s)
                if LAG <= s < UNITS + LAG:
                    transposes(s)
                G, kt = (s - PV_AT) // 16 - 1, (s - PV_AT) % 16 // PV_EVERY
                if 0 <= G < 4 * B and (s - PV_AT) % 16 in range(0, 4 * PV_EVERY, PV_EVERY):
                    pv(G, kt)
                for j in jobs:
                    if s in (j.first, j.step):
                        fill(j, s)
                if s in AHEAD:
                    fill_slot()
            keep_warm(WARM["softmax"])

            pe.wait_ge(s_probs, 1)
            for hf in range(2):
                i = pe.transpose(ps_i[:, P * hf:P * hf + P], probs[:, hf, :, :].rearrange("p s e -> p (s e)"), ident[:, :])
            i.then_inc(s_ptokT, 1)
            for n in range(ROUNDS):
                pe.wait_ge(s_cnt, n + 1)
                pe.matmul(ps_c[:, 0:3], same_e[:, :], cnt[:, 0:3], start=True, stop=True).then_inc(s_tot, 1)
                fill_slot()
            pe.wait_ge(s_cnt, ROUNDS + 1)
            pe.matmul(ps_c[:, 0:1], same_e[:, :], cnt[:, 0:1], start=True, stop=True)
            pe.matmul(ps_c[:, 1:2], earlier[:, :], cnt[:, 1:2], start=True, stop=True).then_inc(s_tot, 1)
            fill_slot()
            pe.wait_ge(s_cnt, ROUNDS + 2)
            pe.matmul(ps_c[:, 0:1], earlier[:, :], cnt[:, 0:1], start=True, stop=True).then_inc(s_tot, 1)
            fill_slot()
            pe.wait_ge(s_pos, 1)
            for hf in range(2):
                i = pe.transpose(ps_i[:, P * hf:P * hf + P], prefix[:, P * hf:P * hf + P], ident[:, :])
            i.then_inc(s_posT, 1)
            fill_slot()
            fill_slot()
            pe.wait_ge(s_route, 1)

            def routes(e, k):
                pe.wait_ge(s_hot, e + 1)
                if not isinstance(e, int) or e:
                    pe.wait_ge(s_idx, e)
                for ch in range(2):
                    for n in range(NT):
                        i = pe.matmul(ps_i[:, 5 * ch:5 * ch + 5], hot[k][:, n, P * ch:P * ch + P], route_e[k][:, n, :],
                                      start=(n == 0), stop=(n == NT - 1))
                i.then_inc(s_ri, 1)

            def turn_gathered(e, k, p):
                pe.wait_ge(s_gath[k], 32 * (p + 1))
                if not isinstance(e, int) or e:
                    pe.wait_ge(s_xlo, e)
                for c in range(DC):
                    for ch in range(2):
                        i = pe.transpose(ps_x[:, C * c + P * ch:C * c + P * ch + P], xg[k][:, ch, P * c:P * c + P], ident[:, :])
                i.then_inc(s_xgt, 1)

            def body(e, k, p, last):
                pe.wait_ge(s_xlo, e + 1)
                for i in range(IC):
                    if i in (0, 4):
                        low_parts(pe, e, 1 + 2 * (i // 4))
                    if i == 2 and not (last and k == 1):
                        routes(e + 1, 1 - k)
                    if not isinstance(p, int) or p or k or i >= len(ps_g):
                        pe.wait_ge(s_hid, IC * e + i - len(ps_g) + 1)
                    for which in range(2):
                        j = 2 * (i // 4) + which
                        for c in range(DC):
                            at = I // 2 * c + P * (i % 4)
                            m = exact(ps_g_of(k, i)[:, C * which:C * which + C], w_hi[k][j][:, at:at + P], w_lo[k][j][:, at:at + P],
                                      x_hi[k][:, c, :], x_lo[k][:, c, :], c == 0, c == DC - 1)
                    m.then_inc(s_gu, 1)
                if not (last and k == 1):
                    turn_gathered(e + 1, 1 - k, p + k)
                low_parts(pe, e, PIECES - 1)
                if not isinstance(p, int) or p or k:
                    pe.wait_ge(s_eo, e)
                for tiles in (range(IC - 1), range(IC - 1, IC)):
                    for ch in range(2):
                        for i in tiles:
                            if ch == 0:
                                pe.wait_ge(s_h, IC * e + i + 1)
                            j, at = 4 + i // 4, D * (i % 4)
                            m = exact((ps_d, ps_c)[ch][:, 0:D], h_hi[:, i, P * ch:P * ch + P], h_lo[:, i, P * ch:P * ch + P],
                                      w_hi[k][j][:, at:at + D], w_lo[k][j][:, at:at + D], i == 0, i == IC - 1)
                m.then_inc(s_dn, 1)

            routes(0, 0)
            while filled[0] < len(slots):
                fill_slot()
            pe.wait_ge(s_sadd, NT)
            turn_gathered(0, 0, 0)
            experts(pe, body)


_OUTS = [((4, 512, 256), "float32")]


def kernel(**inputs):
    import numpy as _np
    import concourse.bacc as _bacc
    from concourse import mybir as _mybir
    from concourse.bass_utils import run_bass_kernel_spmd as _run

    a = {k: _np.asarray(v) for k, v in inputs.items()}
    p = {k[len("L0_xattn_"):]: v for k, v in a.items() if k.startswith("L0_xattn_")}
    f = {k[len("L0_ffn_"):]: v for k, v in a.items() if k.startswith("L0_ffn_")}
    x = a["x"]
    d = x.shape[-1]
    arrays = {
        "x": x.reshape(-1, d), "ctxT": a["ctx_1024"].reshape(-1, d).T, "mask": a["mask_Bx1xSxS2_ik1"][:, 0],
        "adj": p["adj"], "WqT": p["Wq"].T, "bq": p["bq"], "WkT": p["Wk"].T, "bk": p["bk"],
        "WvT": p["Wv"].T, "bv": p["bv"], "WoT": p["Wo"].T, "bo": p["bo"], "gateT": f["gate_w"].T,
        "WgT": f["Wg"].transpose(0, 2, 1), "WuT": f["Wu"].transpose(0, 2, 1), "WdT": f["Wd"].transpose(0, 2, 1),
        "SgT": f["Sg"].T, "SuT": f["Su"].T, "SdT": f["Sd"].T,
    }
    arrays = {k: _np.ascontiguousarray(v) for k, v in arrays.items()}
    nc = _bacc.Bacc("TRN2", target_bir_lowering=False, num_devices=1)
    args = [nc.dram_tensor(f"in_{k}", v.shape, _mybir.dt.from_np(v.dtype), kind="ExternalInput").ap()
            for k, v in arrays.items()]
    out = nc.dram_tensor("out_0", [x.shape[0] * x.shape[1], d], F32, kind="ExternalOutput").ap()
    build(nc, *args, out)
    r = _run(nc, [{f"in_{k}": v for k, v in arrays.items()}], core_ids=[0])
    return r.results[0]["out_0"].reshape(x.shape)
```
